# Optimizing a Trainium2 kernel written in Bass

```python
import numpy as np
import jax
import jax.numpy as jnp

def _softmax(x, axis=-1):
    return jax.nn.softmax(x, axis=axis)

def _gelu(x):
    return jax.nn.gelu(x, approximate=True)

def _silu(x):
    return jax.nn.silu(x)

def _sigmoid(x):
    return jax.nn.sigmoid(x)

def _layernorm(x, axis=-1, eps=1e-05):
    m = jnp.mean(x, axis=axis, keepdims=True)
    v = jnp.var(x, axis=axis, keepdims=True)
    return (x - m) / jnp.sqrt(v + eps)

def _scatter_add(tgt, idx, src, axis=0):
    return tgt.at[idx].add(src)

def _segment_sum(src, seg, n):
    return jax.ops.segment_sum(src, seg, n)
kernel_name = 'mk_cond_resid_d2_seqx_r4_571936'

def setup_inputs(seed: int=0):
    np.random.seed(seed)
    _w = jnp.asarray

    def _rec_inputs():
        import jax
        import jax.numpy as jnp
        _rk = jax.random.key(seed)
        x = 7.22e-05 + 1 * jax.random.normal(jax.random.fold_in(_rk, 1), (8, 256, 1024), jnp.float32)
        _lenS = 256 - jax.random.randint(jax.random.fold_in(_rk, 7), (8,), 0, max(1, 256 // 4) + 1, jnp.int32)
        _lenS2 = 256 - jax.random.randint(jax.random.fold_in(_rk, 8), (8,), 0, max(1, 256 // 4) + 1, jnp.int32)
        itok_B_2_6 = jax.random.randint(jax.random.fold_in(_rk, 11), (8,), 2, 7, jnp.int32)
        itok_B_1_7 = jax.random.randint(jax.random.fold_in(_rk, 12), (8,), 1, 8, jnp.int32)
        return (x, itok_B_2_6, itok_B_1_7)
    x, itok_B_2_6, itok_B_1_7 = _rec_inputs()

    def _L0_cond_setup():
        import jax, jax.numpy as jnp
        import numpy as np
        B, N, H, F = (4, 128, 1024, 2752)
        L, R, RANK = (1, 16, 16)
        SCALE = 0.5
        key = jax.random.key(seed)
        ks = jax.random.split(key, 12)
        nrm = lambda k, shape, fan: jax.random.normal(k, shape, jnp.float32) * fan ** (-0.5)
        inp = {'x': jax.random.normal(ks[0], (B, N, H), jnp.float32), 'W_gate': nrm(ks[1], (F, H), H), 'W_up': nrm(ks[2], (F, H), H), 'W_down': nrm(ks[3], (H, F), F), 'A_gate': nrm(ks[4], (L, R, RANK, H), H), 'B_gate': nrm(ks[5], (L, R, F, RANK), RANK), 'A_up': nrm(ks[6], (L, R, RANK, H), H), 'B_up': nrm(ks[7], (L, R, F, RANK), RANK), 'A_down': nrm(ks[8], (L, R, RANK, F), F), 'B_down': nrm(ks[9], (L, R, H, RANK), RANK), 'lora_indices': jax.random.randint(ks[10], (B,), 0, R), 'layer_idx': 0}
        return inp
    _L0_cond_all = _L0_cond_setup()
    _L0_cond_in = {k: v for k, v in _L0_cond_all.items() if k in ('W_gate', 'W_up', 'W_down', 'A_gate', 'B_gate', 'A_up', 'B_up', 'A_down', 'B_down')}
    del _L0_cond_all

    def _L1_cond_setup():
        import jax, jax.numpy as jnp
        import numpy as np
        B, S, D_IN, D_OUT = (4, 512, 1024, 1024)
        N_ADAPTERS, MAX_RANK = (8, 16)
        key = jax.random.key(seed)
        ks = jax.random.split(key, 7)
        x = jax.random.normal(ks[0], (B, S, D_IN), dtype=jnp.float32)
        weight = jax.random.normal(ks[1], (D_OUT, D_IN), dtype=jnp.float32) * (1.0 / np.sqrt(D_IN))
        bias = jax.random.normal(ks[2], (D_OUT,), dtype=jnp.float32) * 0.01
        lora_a_weights = jax.random.normal(ks[3], (N_ADAPTERS, MAX_RANK, D_IN), dtype=jnp.float32) * (1.0 / np.sqrt(D_IN))
        lora_b_weights = jax.random.normal(ks[4], (N_ADAPTERS, D_OUT, MAX_RANK), dtype=jnp.float32) * 0.02
        scaling_factors = jax.random.uniform(ks[5], (N_ADAPTERS,), dtype=jnp.float32, minval=0.5, maxval=2.0)
        adapter_id = jax.random.randint(ks[6], (B,), 0, N_ADAPTERS, dtype=jnp.int64)
        return {'x': x, 'weight': weight, 'bias': bias, 'lora_a_weights': lora_a_weights, 'lora_b_weights': lora_b_weights, 'scaling_factors': scaling_factors, 'adapter_id': adapter_id}
    _L1_cond_all = _L1_cond_setup()
    _L1_cond_in = {k: v for k, v in _L1_cond_all.items() if k in ('weight', 'bias', 'lora_a_weights', 'lora_b_weights', 'scaling_factors')}
    del _L1_cond_all
    return {'x': x, 'itok_B_2_6': itok_B_2_6, 'itok_B_1_7': itok_B_1_7, 'L0_cond_W_gate': _L0_cond_in['W_gate'], 'L0_cond_W_up': _L0_cond_in['W_up'], 'L0_cond_W_down': _L0_cond_in['W_down'], 'L0_cond_A_gate': _L0_cond_in['A_gate'], 'L0_cond_B_gate': _L0_cond_in['B_gate'], 'L0_cond_A_up': _L0_cond_in['A_up'], 'L0_cond_B_up': _L0_cond_in['B_up'], 'L0_cond_A_down': _L0_cond_in['A_down'], 'L0_cond_B_down': _L0_cond_in['B_down'], 'L1_cond_weight': _L1_cond_in['weight'], 'L1_cond_bias': _L1_cond_in['bias'], 'L1_cond_lora_a_weights': _L1_cond_in['lora_a_weights'], 'L1_cond_lora_b_weights': _L1_cond_in['lora_b_weights'], 'L1_cond_scaling_factors': _L1_cond_in['scaling_factors']}

def reference(x, itok_B_2_6, itok_B_1_7, L0_cond_W_gate, L0_cond_W_up, L0_cond_W_down, L0_cond_A_gate, L0_cond_B_gate, L0_cond_A_up, L0_cond_B_up, L0_cond_A_down, L0_cond_B_down, L1_cond_weight, L1_cond_bias, L1_cond_lora_a_weights, L1_cond_lora_b_weights, L1_cond_scaling_factors):
    import jax
    import jax.numpy as jnp

    def _L0_cond_ref(x, W_gate, W_up, W_down, A_gate, B_gate, A_up, B_up, A_down, B_down, lora_indices, layer_idx):
        import jax, jax.numpy as jnp
        import numpy as np
        B, N, H, F = (4, 128, 1024, 2752)
        L, R, RANK = (1, 16, 16)
        SCALE = 0.5

        def lora_add(base, inp, A, B):
            Ab = A[layer_idx][lora_indices]
            Bb = B[layer_idx][lora_indices]
            t = jnp.einsum('bri,bni->bnr', Ab, inp)
            return base + jnp.einsum('bor,bnr->bno', Bb, t) * SCALE
        gate = lora_add(jnp.einsum('bnh,fh->bnf', x, W_gate), x, A_gate, B_gate)
        up = lora_add(jnp.einsum('bnh,fh->bnf', x, W_up), x, A_up, B_up)
        act = jax.nn.silu(gate) * up
        down = lora_add(jnp.einsum('bnf,hf->bnh', act, W_down), act, A_down, B_down)
        return down

    def _L1_cond_ref(x, weight, bias, lora_a_weights, lora_b_weights, scaling_factors, adapter_id):
        import jax, jax.numpy as jnp
        import numpy as np
        B, S, D_IN, D_OUT = (4, 512, 1024, 1024)
        N_ADAPTERS, MAX_RANK = (8, 16)
        base = jnp.einsum('bsi,oi->bso', x, weight) + bias
        a_sel = lora_a_weights[adapter_id]
        b_sel = lora_b_weights[adapter_id]
        scale = scaling_factors[adapter_id]
        low = jnp.einsum('bsi,bri->bsr', x, a_sel)
        delta = jnp.einsum('bsr,bor->bso', low, b_sel)
        return base + scale[:, None, None] * delta
    x = x + _L0_cond_ref(x, L0_cond_W_gate, L0_cond_W_up, L0_cond_W_down, L0_cond_A_gate, L0_cond_B_gate, L0_cond_A_up, L0_cond_B_up, L0_cond_A_down, L0_cond_B_down, itok_B_2_6, 0)
    x = x + _L1_cond_ref(x, L1_cond_weight, L1_cond_bias, L1_cond_lora_a_weights, L1_cond_lora_b_weights, L1_cond_scaling_factors, itok_B_1_7)
    return x

_drawn_inputs = setup_inputs


def setup_inputs(seed=0):
    import zlib

    import numpy as np

    out = dict(_drawn_inputs(seed))
    spreads = {}
    factors = {'L1_cond_bias': 8.0, 'L1_cond_scaling_factors': 2.951}
    for name, (base, spread) in spreads.items():
        noise = np.random.default_rng([zlib.crc32(name.encode()), seed]).standard_normal(out[name].shape)
        drawn = base * np.exp(spread * noise) if base else spread * noise
        out[name] = jnp.asarray(drawn.astype(out[name].dtype))
    for name, factor in factors.items():
        out[name] = (out[name] * factor).astype(out[name].dtype)
    return out
```

```python
from contextlib import ExitStack

import concourse.bass as bass
from concourse import mybir

F32 = mybir.dt.float32
F32R = mybir.dt.float32r
ACT = mybir.ActivationFunctionType
ALU = mybir.AluOpType

P = 128
Q = 32
NQ = P // Q
RAW = 4
TURNED = 2
START = 1
BEFORE, AFTER = "before", "after"


class Tally:

    def __init__(self, before, body, after, turns):
        self.before, self.body, self.turns = before, body, turns
        self.total = before + turns * body + after

    def at(self, h, s, n):
        if s is BEFORE:
            return h * self.total + n
        if s is AFTER:
            return h * self.total + (self.before + self.turns * self.body + n)
        return h * self.total + s * self.body + (self.before + n)


def build(nc, x, l0_index, l1_index, w_gate, w_up, w_down, a_gate, b_gate, a_up, b_up, a_down, b_down,
          w_out, bias_in, a_out, b_out, scale_in, out):
    NB, NS, H = x.shape
    F = w_gate.shape[0]
    R = a_gate.shape[2]
    HALVES = 2
    BH = NB // HALVES
    T = BH * NS
    TT = 512
    NT = T // TT
    KT = H // P
    HQ = H // NQ
    FB = 256
    TURNS = F // FB - 1
    MR = F % FB // NQ * NQ // 2
    QR = MR // Q
    ADDS = KT + 1
    assert (NS, TT, 2 * R, F % FB, F // FB) == (256, 2 * NS, Q, 2 * MR, 10) and MR == 96
    assert l0_index.shape[0] == NB and NT == 2 and KT == 8

    tokens = x.rearrange("b s h -> (b s) h")
    out_tokens = out.rearrange("b s h -> (b s) h")

    with ExitStack() as ctx:
        def sbuf(name, shape, dtype=F32):
            return ctx.enter_context(nc.sbuf_tensor(name, shape, dtype))

        def sem(name):
            return ctx.enter_context(nc.semaphore(name))

        X = sbuf("X", [P, 2, KT, T], F32R)
        acc = sbuf("acc", [P, ADDS, T])
        act = sbuf("act", [P, 2, 2, T], F32R)
        Wd = sbuf("Wd", [P, 2, 2, KT, P], F32R)
        Wk = [sbuf(f"Wk{j}", [P, 2, KT, P], F32R) for j in range(2)]
        raw = [sbuf(f"raw{j}", [P, 1024]) for j in range(RAW)]
        turned = [sbuf(f"turned{j}", [P, 1024]) for j in range(TURNED)]
        work = [sbuf(f"work{j}", [P, T]) for j in range(2)]
        Bf = sbuf("Bf", [96, 2, 2, 2, P], F32R)
        Ad_raw = sbuf("Ad_raw", [2 * Q, FB])
        Ad_turned = sbuf("Ad_turned", [P, 2, 2, Q])
        Ad = sbuf("Ad", [P, 2, 2, 2, Q], F32R)
        Tm = [sbuf(f"Tm{j}", [96, T], F32R) for j in range(2)]
        stage = [sbuf(f"stage{j}", [P, 16, 64]) for j in range(2)]
        bias = sbuf("bias", [P, KT])
        scale_row = sbuf("scale_row", [Q, BH])
        pick = sbuf("pick", [Q, BH])
        pick_half = sbuf("pick_half", [Q, BH])
        pick_scale = sbuf("pick_scale", [Q, BH])

        ps = [ctx.enter_context(nc.psum_tensor(f"ps{j}", [P, T], F32)) for j in range(4)]

        raw_full = [sem(f"raw_full{j}") for j in range(RAW)]
        turned_full = [sem(f"turned_full{j}") for j in range(TURNED)]
        hi_full = [sem(f"hi_full{j}") for j in range(TURNED)]
        lo_full = [sem(f"lo_full{j}") for j in range(TURNED)]
        wk_used = [[sem(f"wk_used{j}{g}") for g in range(2)] for j in range(2)]
        ad_loaded, ad_turned, ad_hi, ad_full = (sem(n) for n in ("ad_loaded", "ad_turned", "ad_hi", "ad_full"))
        unit_done = [[sem(f"unit_done{w}{c}") for c in range(2)] for w in range(2)]
        silu_done = [sem(f"silu_done{c}") for c in range(2)]
        mult_done = [sem(f"mult_done{c}") for c in range(2)]
        act_hi = [sem(f"act_hi{c}") for c in range(2)]
        act_full = [sem(f"act_full{c}") for c in range(2)]
        t_copied, t_summed, t_masked, t_hi, t_full = (sem(n) for n in (
            "t_copied", "t_summed", "t_masked", "t_hi", "t_full"))
        down_done, down_added = sem("down_done"), sem("down_added")
        acc_set, x1_hi, x1_full = sem("acc_set"), sem("x1_hi"), sem("x1_full")
        out_done, out_added, out_turned = (sem(n) for n in ("out_done", "out_added", "out_turned"))
        out_stored = [sem(f"out_stored{m}") for m in range(2)]
        bias_loaded, pick_set, pick_ready = (sem(n) for n in ("bias_loaded", "pick_set", "pick_ready"))

        BLOCKS = TURNS + 2
        ITEMS_BEFORE, TURN_ITEMS, ITEMS_AFTER = 16, 8, 24
        X_PIECES = 8
        AGU = [0, 5]
        X_AT = [1, 2, 3, 4, 6, 7, 8, 9]
        AL = 12
        DMAS = 4
        FIRST_ITEMS = ["Agu0", "x0", "x1", "x2", "x3", "Agu1", "x4", "x5", "x6", "x7", "G", "Bg", "U", "Bu"]
        WK_USED = [1 + 2 * BLOCKS + KT // 2, 1 + 2 * BLOCKS + 1 + KT // 2]
        DOWNS = BLOCKS * ADDS
        T_CHAINS = 4

        def in_ring(ring, h, s, n):
            return n % ring, Tally(ITEMS_BEFORE // ring, TURN_ITEMS // ring, ITEMS_AFTER // ring, TURNS).at(
                h, s, n // ring)

        def turned_at(h, s, n):
            return in_ring(TURNED, h, s, n)

        def by_vector(n, item):
            return item[0] == "x" and n % 2 == 0

        def item_full(eng, h, s, n, granules=2):
            j, before = turned_at(h, s, n)
            eng.wait_ge(lo_full[j], START + before * 2 + granules)

        def down_pair(b, i):
            if isinstance(b, int) and b == BLOCKS - 1:
                return 2 if i == 0 else (2 + i) % 4
            return 2 + i % 2

        block = ctx.enter_context(nc.Block())

        @block.sync
        def _(sp):
            with sp.Fori(0, HALVES) as h:
                def indices(table, rows):
                    flat = table.rearrange("(o n) -> o n", o=1)
                    return [sp.value_load(flat[:, bass.ds(h * BH + b, 1)], min_val=0, max_val=rows - 1)
                            for b in range(BH)]

                l0 = indices(l0_index, a_gate.shape[1])
                l1 = indices(l1_index, a_out.shape[0])

                def slot(s, n):
                    last = n - RAW
                    if s is BEFORE and last < 0:
                        for j in range(TURNED):
                            sp.wait_ge(turned_full[j], START + turned_at(h, BEFORE, 0)[1])
                    else:
                        j, before = turned_at(h, s, last)
                        sp.wait_ge(turned_full[j], START + before + 1)
                    return raw[n % RAW], raw_full[n % RAW]

                def quadrants(nq):
                    return [(q, 0, 8) for q in range(nq)] if nq == 4 else [(0, 0, 8), (1, 0, 8), (2, 0, 4), (2, 4, 8)]

                def load_rows(s, n, w, group, step, nq):
                    buf, full = slot(s, n)
                    rows = w.rearrange("(g i) m -> i g m", i=Q)
                    for c in range(NQ):
                        sp.dma_start(buf[c * Q:(c + 1) * Q, 0:nq * HQ].rearrange("i (q m) -> i q m", q=nq),
                                     rows[:, bass.ds(group, nq, step), c * HQ:(c + 1) * HQ]).then_inc(full, 16)

                def load_down(s, n, e, f0, nq):
                    buf, full = slot(s, n)
                    rows = w_down.rearrange("(g i) f -> i g f", i=Q)
                    for q, lo, hi in quadrants(nq):
                        sp.dma_start(buf[q * Q:(q + 1) * Q, 128 * lo:128 * hi].rearrange("i (g f) -> i g f", f=64),
                                     rows[:, 16 * e + 2 * lo:16 * e + 2 * hi, bass.ds(f0 + q * 64, 64)]
                                     ).then_inc(full, 16)

                def load_b(s, n, b_all, f0, each):
                    buf, full = slot(s, n)
                    for b in range(BH):
                        src = b_all[0, bass.ds(l0[b], 1), bass.ds(f0, Q * each), :]
                        sp.dma_start(buf[0:Q, b * 128:b * 128 + each * R],
                                     src.rearrange("o (i j) r -> (o i) (j r)", i=Q)).then_inc(full, 16)

                def load_b_pair(s, n, b_all, index, p):
                    buf, full = slot(s, n)
                    for b in range(2):
                        src = b_all[bass.ds(index[2 * p + b], 1), :, :].rearrange("o (i j) r -> (o i) (j r)", i=Q)
                        for m in range(2):
                            sp.dma_start(buf[0:Q, b * 512 + m * 256:b * 512 + (m + 1) * 256],
                                         src[:, m * 256:(m + 1) * 256]).then_inc(full, 16)

                def load_a(s, n, parts):
                    buf, full = slot(s, n)
                    for g, (a_all, index) in enumerate(parts):
                        sp.dma_start(buf[g * R:(g + 1) * R, :],
                                     a_all[bass.ds(index, 1), :, :].rearrange("o r m -> (o r) m")
                                     ).then_inc(full, 16)

                def load_ad(f0, nq):
                    for b in range(BH):
                        src = a_down[0, bass.ds(l0[b], 1), :, bass.ds(f0, nq * 64)]
                        sp.dma_start(Ad_raw[b * R:(b + 1) * R, 0:nq * 64],
                                     src.rearrange("o r m -> (o r) m")).then_inc(ad_loaded, 16)

                def load_turn(s, b, nq):
                    load_down(s, 0, 0, b * FB, NQ)
                    load_down(s, 1, 1, b * FB, NQ)
                    sp.wait_ge(ad_turned, START + h * BLOCKS + b)
                    load_ad(b * FB, NQ)
                    load_rows(s, 2, w_gate, (b + 1) * (FB // Q), 2, nq)
                    load_b(s, 3, b_gate, (b + 1) * FB, 2 * nq)
                    load_rows(s, 4, w_up, (b + 1) * (FB // Q), 2, nq)
                    load_b(s, 5, b_up, (b + 1) * FB, 2 * nq)
                    load_rows(s, 6, w_gate, (b + 1) * (FB // Q) + 1, 2, nq)
                    load_rows(s, 7, w_up, (b + 1) * (FB // Q) + 1, 2, nq)

                for p in range(NT):
                    load_a(BEFORE, AGU[p], [(a, l0[2 * p + b]) for a in (a_gate[0], a_up[0]) for b in range(2)])
                    for n in range(4 * p, 4 * p + 4):
                        first_col, first_token = n // 4 * 128, n % 4 * 256
                        buf, full = slot(BEFORE, X_AT[n])
                        for c in range(NQ):
                            col = c * HQ + first_col
                            src = tokens[bass.ds(h * T + first_token, 256), col:col + 128]
                            sp.dma_start(buf[c * Q:(c + 1) * Q, :].rearrange("i (t m) -> i t m", t=8),
                                         src.rearrange("(t i) m -> i t m", i=Q)).then_inc(full, 16)
                load_rows(BEFORE, 10, w_gate, 0, 2, NQ)
                load_b(BEFORE, 11, b_gate, 0, 8)
                load_rows(BEFORE, 12, w_up, 0, 2, NQ)
                load_b(BEFORE, 13, b_up, 0, 8)
                load_rows(BEFORE, 14, w_gate, 1, 2, NQ)
                load_rows(BEFORE, 15, w_up, 1, 2, NQ)
                with sp.Fori(0, TURNS) as s:
                    load_turn(s, s, NQ)
                load_turn(AFTER, TURNS, QR)
                load_down(AFTER, 8, 0, (BLOCKS - 1) * FB, QR)
                load_down(AFTER, 9, 1, (BLOCKS - 1) * FB, QR)
                load_b_pair(AFTER, 10, b_down[0], l0, 0)
                load_b_pair(AFTER, 11, b_down[0], l0, 1)
                load_a(AFTER, AL, [(a_out, l1[b]) for b in range(BH)])
                sp.wait_ge(ad_turned, START + h * BLOCKS + (BLOCKS - 1))
                buf, full = slot(AFTER, 13)
                load_ad((BLOCKS - 1) * FB, QR)
                for b in range(BH):
                    factor = scale_in.rearrange("(n o) -> n o", o=1)[bass.ds(l1[b], 1), :]
                    sp.dma_start(buf[0:Q, b:b + 1], factor.to_broadcast([Q, 1]),
                                 allow_slow_non_contiguous=True).then_inc(full, 16)
                for k in range(KT):
                    if k == 2:
                        load_b_pair(AFTER, 16, b_out, l1, 0)
                        load_b_pair(AFTER, 17, b_out, l1, 1)
                    load_rows(AFTER, 14 + k + (2 if k >= 2 else 0), w_out, k, KT, NQ)

        def places(item, g, j, m, k_out=0):
            src, ks = turned[j], slice(4 * g, 4 * g + 4)
            if item in ("G", "U", "O"):
                wk = Wk[{"G": 0, "U": 1, "O": k_out % 2}[item]]
                return (src[:, 0:KT * m].rearrange("p (k m) -> p k m", k=KT)[:, ks, :],
                        [wk[:, 0, ks, 0:m]], wk[:, 1, ks, 0:m])
            if item in ("Agu0", "Agu1", "Al"):
                wk = Wk[0 if item == "Agu0" else 1][:, 0, ks, :].rearrange("p k (w l r) -> p k w l r", w=2, l=2)
                return (src[:, 0:512].rearrange("p (k w r) -> p k w r", k=KT, w=2)[:, ks, :, :],
                        [wk[:, :, :, 0, :]], wk[:, :, :, 1, :])
            if item in ("D0", "D1"):
                e = int(item[1])
                hi_lo = [Wd[0:m, g, l, :, e * 64:(e + 1) * 64].rearrange("p k (q i) -> p q k i", q=2)
                         for l in range(2)]
                return (src[0:m, g * 512:(g + 1) * 512].rearrange("p (q k i) -> p q k i", q=2, k=KT),
                        [hi_lo[0]], hi_lo[1])
            if item in ("Bg", "Bu"):
                w, nq = "gu".index(item[1]), m // Q
                rows = [Bf[r * Q:(r + 1) * Q, w, g, :, 0:m].rearrange("p w (q i) -> p w q i", q=nq)
                        for r in range(3)]
                return (src[0:Q, 0:2 * FB].rearrange("p (w q c i) -> p w q c i", w=2, q=NQ, c=2)[:, :, 0:nq, g, :],
                        rows[0:2], rows[2])
            if item[0] == "x":
                n = int(item[1])
                ks, ts = slice(n // 4 * 4 + 2 * g, n // 4 * 4 + 2 * g + 2), slice(n % 4 * 256, n % 4 * 256 + 256)
                return (src[:, :].rearrange("p (k t) -> p k t", k=4)[:, 2 * g:2 * g + 2, :],
                        [X[:, 0, ks, ts]], X[:, 1, ks, ts])
            if item == "scale":
                return src[0:Q, 2 * g:2 * g + 2], [scale_row[:, 2 * g:2 * g + 2]], pick_scale[:, 2 * g:2 * g + 2]
            p = int(item[2])
            home = Wk[0][:, p] if item[1] == "d" else Wd[:, 0, p]
            rows = [home[r * Q:(r + 1) * Q, ks, :].rearrange("p k (q i) -> p q k i", q=NQ) for r in range(3)]
            return (src[0:Q, :].rearrange("p (q k i) -> p q k i", q=NQ, k=KT)[:, :, ks, :], rows[0:2], rows[2])

        @block.scalar
        def _(act_eng):
            eng = act_eng
            for sem_ in (*silu_done, *out_stored):
                eng.sem_inc(sem_, START)
            with eng.Fori(0, HALVES) as h:
                def home_free(item, g, n):
                    if item in ("Agu0", "Agu1"):
                        p = int(item[3])
                        eng.wait_ge(wk_used[p][g], START + h * WK_USED[p])
                    elif item[0] == "x":
                        eng.wait_ge(wk_used[1][int(item[1]) // 4], START + h * WK_USED[1])
                    elif item == "G":
                        eng.wait_ge(wk_used[0][g], START + h * WK_USED[0] + n + 1)
                    elif item == "U":
                        eng.wait_ge(wk_used[1][g], START + h * WK_USED[1] + n + 1)
                    elif item in ("Bg", "Bu"):
                        eng.wait_ge(unit_done["gu".index(item[1])][g], START + h * BLOCKS + n)
                    elif item in ("D0", "D1"):
                        eng.wait_ge(down_done, START + h * DOWNS + n * ADDS)
                        eng.wait_ge(out_done, START + h * KT)
                    elif item in ("Bd0", "Bd1"):
                        for gg in range(2):
                            eng.wait_ge(wk_used[0][gg], START + h * WK_USED[0] + (1 + 2 * BLOCKS))
                    elif item == "Al":
                        eng.wait_ge(wk_used[1][g], START + h * WK_USED[1] + (1 + 2 * BLOCKS))
                    elif item == "O":
                        eng.wait_ge(wk_used[n % 2][g], START + h * WK_USED[n % 2] + (1 + n % 2 + 2 * BLOCKS + n // 2))
                        eng.wait_ge(down_done, START + h * DOWNS + DOWNS)
                    elif item in ("Bl0", "Bl1"):
                        eng.wait_ge(down_done, START + h * DOWNS + DOWNS)

                def hi(s, n, item, at=0, m=P):
                    j, before = turned_at(h, s, n)
                    eng.wait_ge(turned_full[j], START + before + 1)
                    for g in range(2):
                        home_free(item, g, at)
                        src, homes, _ = places(item, g, j, m, at)
                        for home in homes:
                            last = nc.scalar.activation(home, src, ACT.Copy)
                        last.then_inc(hi_full[j], 1)

                def silu(c, b):
                    eng.wait_ge(unit_done[0][c], START + h * BLOCKS + b + 1)
                    eng.wait_ge(act_full[c], START + h * BLOCKS + b)
                    eng.wait_ge(t_full, h * T_CHAINS + (c + 1))
                    nc.scalar.activation(work[c][:, :], ps[2 * c][:, :], ACT.Silu).then_inc(silu_done[c], 1)

                def act_high(c, b):
                    eng.wait_ge(mult_done[c], START + h * BLOCKS + b + 1)
                    eng.wait_ge(down_done, START + h * DOWNS + b * ADDS)
                    nc.scalar.activation(act[:, c, 0, :], work[c][:, :], ACT.Copy).then_inc(act_hi[c], 1)

                def ad_high(b, m):
                    eng.wait_ge(ad_turned, START + h * BLOCKS + b + 1)
                    eng.wait_ge(down_done, START + h * DOWNS + b * ADDS)
                    nc.scalar.activation(Ad[0:m, :, :, 0, :], Ad_turned[0:m, :, :, :], ACT.Copy).then_inc(ad_hi, 1)

                def t_copy(src, w):
                    nc.scalar.activation(work[w][0:Q, :], src, ACT.Copy).then_inc(t_copied, 1)

                def t_high(w, n):
                    eng.wait_ge(t_masked, h * T_CHAINS + n + 1)
                    nc.scalar.activation(Tm[w][0:Q, :], work[w][0:Q, :], ACT.Copy)
                    nc.scalar.activation(Tm[w][2 * Q:3 * Q, :], work[w][0:Q, :], ACT.Copy).then_inc(t_hi, 1)

                def turn(s, b, m):
                    act_high(0, b)
                    hi(s, 0, "D0", b)
                    hi(s, 1, "D1", b)
                    ad_high(b, P)
                    hi(s, 2, "G", 2 * b + 2, m)
                    silu(1, b)
                    hi(s, 3, "Bg", b + 1, m)
                    hi(s, 4, "U", 2 * b + 2, m)
                    act_high(1, b)
                    hi(s, 5, "Bu", b + 1, m)
                    silu(0, b + 1)
                    hi(s, 6, "G", 2 * b + 3, m)
                    hi(s, 7, "U", 2 * b + 3, m)

                for n, item in enumerate(FIRST_ITEMS):
                    hi(BEFORE, n, item)
                eng.wait_ge(wk_used[1][1], START + h * WK_USED[1] + 1)
                t_copy(ps[2][Q:2 * Q, :], 0)
                t_copy(ps[2][3 * Q:4 * Q, :], 1)
                t_high(0, 0)
                t_high(1, 1)
                silu(0, 0)
                hi(BEFORE, 14, "G", 1)
                hi(BEFORE, 15, "U", 1)
                with eng.Fori(0, TURNS) as s:
                    turn(s, s, P)
                turn(AFTER, TURNS, MR)

                act_high(0, BLOCKS - 1)
                hi(AFTER, 8, "D0", BLOCKS - 1, MR)
                hi(AFTER, 9, "D1", BLOCKS - 1, MR)
                ad_high(BLOCKS - 1, MR)
                silu(1, BLOCKS - 1)
                hi(AFTER, 10, "Bd0")
                hi(AFTER, 11, "Bd1")
                act_high(1, BLOCKS - 1)
                hi(AFTER, AL, "Al")
                hi(AFTER, 13, "scale")
                last_block = h * DOWNS + (BLOCKS - 1) * ADDS
                eng.wait_ge(down_added, START + last_block + 1)
                eng.wait_ge(act_full[1], START + h * BLOCKS + BLOCKS)
                t_copy(acc[Q:2 * Q, KT, :], 1)
                t_high(1, 2)
                for k in range(KT):
                    eng.wait_ge(down_added, START + last_block + 2 + k)
                    nc.scalar.activation(X[:, 0, k, :], acc[:, k, :], ACT.Copy).then_inc(x1_hi, 1)
                hi(AFTER, 14, "O", 0)
                eng.wait_ge(wk_used[1][1], START + h * WK_USED[1] + (2 + 2 * BLOCKS))
                t_copy(ps[3][Q:2 * Q, :], 0)
                hi(AFTER, 15, "O", 1)
                hi(AFTER, 16, "Bl0")
                hi(AFTER, 17, "Bl1")
                t_high(0, 3)

                def store(pair):
                    for m in range(2):
                        eng.wait_ge(out_turned, START + h * KT + (2 * pair + m + 1))
                        for q in range(NQ):
                            col = q * HQ + pair * 2 * Q
                            rows = out_tokens[bass.ds(h * T + m * TT, TT), col:col + 2 * Q]
                            eng.dma_start(rows.rearrange("(t i) m -> i t m", i=Q),
                                          stage[m][q * Q:(q + 1) * Q, :, :]).then_inc(out_stored[m], 16)

                for k in range(KT):
                    if k + 2 < KT:
                        hi(AFTER, 18 + k, "O", k + 2)
                    if k % 2 and k > 1:
                        store((k - 3) // 2)
                store(KT // 2 - 1)
            for m in range(2):
                eng.wait_ge(out_stored[m], START + HALVES * (KT // 2) * NQ * 16)

        @block.gpsimd
        def _(eng):
            for sem_ in (*lo_full, ad_full):
                eng.sem_inc(sem_, START)
            for q in range(NQ):
                eng.dma_start(bias[q * Q:(q + 1) * Q, :],
                              bias_in.rearrange("(q k i) -> q i k", q=NQ, k=KT)[q],
                              allow_slow_non_contiguous=True).then_inc(bias_loaded, 16)
            eng.memset(pick[:, :], 1.0).then_inc(pick_set, 1)
            eng.wait_ge(pick_set, 1)
            parity = pick[:, :].rearrange("p (w b) -> p w b", b=2)
            eng.affine_select(out=parity[:, :, 0], in_=parity[:, :, 0], compare_op=ALU.is_ge, fill=0.0,
                              base=R - 1, pattern=[[0, 2]], channel_multiplier=-1).then_inc(pick_set, 1)
            eng.affine_select(out=parity[:, :, 1], in_=parity[:, :, 1], compare_op=ALU.is_ge, fill=0.0,
                              base=-R, pattern=[[0, 2]], channel_multiplier=1).then_inc(pick_set, 1)
            eng.wait_ge(pick_set, 3)
            nc.gpsimd.tensor_scalar(pick_half[:, :], pick[:, :], 0.5, None, ALU.mult).then_inc(pick_ready, 1)
            with eng.Fori(0, HALVES) as h:
                def lo(s, n, item, at=0, m=P):
                    j, before = turned_at(h, s, n)
                    across = item[0] == "B"
                    if across:
                        item_full(eng, h, s, n - 1)
                        if item == "Bd0":
                            eng.wait_ge(ad_full, START + h * BLOCKS + BLOCKS)
                    for g in range(2):
                        eng.wait_ge(hi_full[j], before * 2 + (g + 1))
                        src, homes, home = places(item, g, j, m, at)
                        if item == "scale":
                            nc.gpsimd.tensor_tensor(home, homes[0], pick[:, 2 * g:2 * g + 2],
                                                    ALU.mult).then_inc(lo_full[j], 1)
                        else:
                            nc.gpsimd.tensor_tensor(home, src, homes[0].bitcast(F32),
                                                    ALU.subtract).then_inc(lo_full[j], 1)
                        if across:
                            item_full(eng, h, s, n, granules=g + 1)

                def ad_low(b, m):
                    eng.wait_ge(ad_hi, h * BLOCKS + b + 1)
                    nc.gpsimd.tensor_tensor(Ad[0:m, :, :, 1, :], Ad_turned[0:m, :, :, :],
                                            Ad[0:m, :, :, 0, :].bitcast(F32), ALU.subtract).then_inc(ad_full, 1)

                def x1_low(k):
                    eng.wait_ge(x1_hi, h * KT + k + 1)
                    nc.gpsimd.tensor_tensor(X[:, 1, k, :], acc[:, k, :], X[:, 0, k, :].bitcast(F32),
                                            ALU.subtract).then_inc(x1_full, 1)

                def acc_start(ks):
                    for k in ks:
                        nc.gpsimd.tensor_tensor(acc[:, k, :], X[:, 0, k, :].bitcast(F32),
                                                X[:, 1, k, :].bitcast(F32), ALU.add).then_inc(acc_set, 1)

                def turn(s, b, m):
                    lo(s, 0, "D0")
                    lo(s, 1, "D1")
                    ad_low(b, P)
                    for n, item in enumerate(("G", "Bg", "U", "Bu", "G", "U")):
                        lo(s, 2 + n, item, m=m)

                for n, item in enumerate(FIRST_ITEMS):
                    if not by_vector(n, item):
                        lo(BEFORE, n, item)
                eng.wait_ge(out_turned, START + h * KT)
                for n in X_AT[-2:]:
                    item_full(eng, h, BEFORE, n)
                acc_start(range(0, 4))
                lo(BEFORE, 14, "G")
                acc_start(range(4, 6))
                lo(BEFORE, 15, "U")
                acc_start(range(6, 8))
                with eng.Fori(0, TURNS) as s:
                    turn(s, s, P)
                turn(AFTER, TURNS, MR)
                lo(AFTER, 8, "D0", m=MR)
                lo(AFTER, 9, "D1", m=MR)
                ad_low(BLOCKS - 1, MR)
                lo(AFTER, 10, "Bd0")
                lo(AFTER, 11, "Bd1")
                lo(AFTER, AL, "Al")
                lo(AFTER, 13, "scale")
                for k in range(KT):
                    x1_low(k)
                lo(AFTER, 14, "O", 0)
                lo(AFTER, 15, "O", 1)
                lo(AFTER, 16, "Bl0")
                lo(AFTER, 17, "Bl1")
                for k in range(2, KT):
                    lo(AFTER, 16 + k, "O", k)

        @block.vector
        def _(eng):
            for sem_ in (*turned_full, ad_turned, *act_full, *mult_done, down_added, out_turned, out_added):
                eng.sem_inc(sem_, START)
            with eng.Fori(0, HALVES) as h:
                def turn_item(s, n, item, nq=NQ):
                    j, before = turned_at(h, s, n)
                    jr, loaded = in_ring(RAW, h, s, n)
                    eng.wait_ge(raw_full[jr], (loaded + 1) * (DMAS * 16))
                    eng.wait_ge(lo_full[j], START + before * 2)
                    src, dst = raw[jr], turned[j]
                    if item in ("G", "U", "O"):
                        last = nc.vector.transpose(
                            dst[:, 0:KT * nq * Q].rearrange("p (k q i) -> p k q i", k=KT, q=nq),
                            src[:, 0:nq * HQ].rearrange("p (q k i) -> p k q i", q=nq, k=KT))
                    elif item in ("Agu0", "Agu1", "Al"):
                        for w in range(2):
                            for q in range(NQ):
                                last = nc.vector.transpose(
                                    dst[q * Q:(q + 1) * Q, 0:512].rearrange(
                                        "p (k w i) -> p k w i", k=KT, w=2)[:, :, w, :],
                                    src[w * Q:(w + 1) * Q, q * HQ:(q + 1) * HQ].rearrange(
                                        "p (k i) -> p k i", k=KT))
                    elif item[0] == "x":
                        last = nc.vector.transpose(dst[:, :].rearrange("p (k t i) -> p k t i", k=4, t=8),
                                                   src[:, :].rearrange("p (t k i) -> p k t i", t=8, k=4))
                    elif item in ("D0", "D1"):
                        last = nc.vector.transpose(
                            dst[0:nq * Q, :].rearrange("p (c g i) -> p c g i", c=2, g=16),
                            src[0:nq * Q, :].rearrange("p (g c i) -> p c g i", g=16, c=2))
                    elif item in ("Bg", "Bu"):
                        each = 2 * nq
                        for w in range(NT):
                            last = nc.vector.transpose(
                                dst[0:Q, w * FB:w * FB + Q * each].rearrange("p (i j) -> p j i", j=each),
                                src[0:Q, w * FB:(w + 1) * FB].rearrange("p (b j r) -> p j b r", b=2, r=R)[
                                    :, 0:each, :, :])
                    elif item == "scale":
                        last = nc.vector.tensor_copy(dst[0:Q, 0:BH], src[0:Q, 0:BH])
                    else:
                        last = nc.vector.transpose(
                            dst[0:Q, :].rearrange("p (i j) -> p j i", j=Q),
                            src[0:Q, :].rearrange("p (b j r) -> p j b r", b=2, r=R))
                    last.then_inc(turned_full[j], 1)

                def item_low(n, item):
                    j, before = turned_at(h, BEFORE, n)
                    for g in range(2):
                        eng.wait_ge(hi_full[j], before * 2 + (g + 1))
                        src, homes, home = places(item, g, j, P)
                        nc.vector.tensor_tensor(home, src, homes[0].bitcast(F32), ALU.subtract
                                                ).then_inc(lo_full[j], 1)

                def turn_ad(b, nq):
                    eng.wait_ge(ad_loaded, (h * BLOCKS + b + 1) * BH * 16)
                    eng.wait_ge(ad_full, START + h * BLOCKS + b)
                    for w in range(NT):
                        for q in range(nq):
                            last = nc.vector.transpose(
                                Ad_turned[q * Q:(q + 1) * Q, :, w, :],
                                Ad_raw[w * Q:(w + 1) * Q, q * 64:(q + 1) * 64].rearrange("p (c i) -> p c i", c=2))
                    last.then_inc(ad_turned, 1)

                def multiply(c, b):
                    eng.wait_ge(unit_done[1][c], START + h * BLOCKS + b + 1)
                    eng.wait_ge(silu_done[c], START + h * BLOCKS + b + 1)
                    nc.vector.tensor_tensor(work[c][:, :], work[c][:, :], ps[2 * c + 1][:, :], ALU.mult
                                            ).then_inc(mult_done[c], 1)

                def act_low(c, b):
                    eng.wait_ge(act_hi[c], h * BLOCKS + b + 1)
                    nc.vector.tensor_tensor(act[:, c, 1, :], work[c][:, :], act[:, c, 0, :].bitcast(F32),
                                            ALU.subtract).then_inc(act_full[c], 1)

                def t_sum(src, w, n, factors):
                    eng.wait_ge(t_copied, h * T_CHAINS + n + 1)
                    nc.vector.tensor_tensor(work[w][0:Q, :], work[w][0:Q, :], src, ALU.add).then_inc(t_summed, 1)
                    eng.wait_ge(t_summed, h * T_CHAINS + n + 1)
                    for b in range(BH):
                        one = work[w][0:Q, b * NS:(b + 1) * NS]
                        last = nc.vector.tensor_scalar(one, one, factors[:, b:b + 1], None, ALU.mult)
                    last.then_inc(t_masked, 1)

                def t_low(w, n):
                    eng.wait_ge(t_hi, h * T_CHAINS + n + 1)
                    nc.vector.tensor_tensor(Tm[w][Q:2 * Q, :], work[w][0:Q, :], Tm[w][0:Q, :].bitcast(F32),
                                            ALU.subtract).then_inc(t_full, 1)

                def add_down(b, i):
                    base = h * DOWNS + b * ADDS
                    pair = down_pair(b, i)
                    eng.wait_ge(down_done, START + base + i + 1)
                    dst = acc[0:2 * Q, KT, :] if i == 0 else acc[:, i - 1, :]
                    src = ps[pair][0:2 * Q, :] if i == 0 else ps[pair][:, :]
                    nc.vector.tensor_tensor(dst, dst, src, ALU.add).then_inc(down_added, 1)

                def turn(s, b, nq):
                    act_low(0, b)
                    turn_item(s, 0, "D0")
                    turn_item(s, 1, "D1")
                    turn_ad(b, NQ)
                    turn_item(s, 2, "G", nq)
                    turn_item(s, 3, "Bg", nq)
                    turn_item(s, 4, "U", nq)
                    multiply(1, b)
                    act_low(1, b)
                    turn_item(s, 5, "Bu", nq)
                    turn_item(s, 6, "G", nq)
                    turn_item(s, 7, "U", nq)
                    multiply(0, b + 1)
                    eng.wait_ge(down_added, START + h * DOWNS + b * ADDS)
                    eng.wait_ge(acc_set, h * (KT + 1) + (KT + 1))
                    for i in range(ADDS):
                        add_down(b, i)

                eng.wait_ge(out_turned, START + h * KT)
                nc.vector.memset(acc[0:2 * Q, KT, :], 0.0).then_inc(acc_set, 1)
                for n, item in enumerate(FIRST_ITEMS):
                    turn_item(BEFORE, n, item)
                    if n and by_vector(n - 1, FIRST_ITEMS[n - 1]):
                        item_low(n - 1, FIRST_ITEMS[n - 1])
                eng.wait_ge(pick_ready, 1)
                t_sum(ps[2][0:Q, :], 0, 0, pick_half)
                t_sum(ps[2][2 * Q:3 * Q, :], 1, 1, pick_half)
                t_low(0, 0)
                t_low(1, 1)
                turn_item(BEFORE, 14, "G")
                turn_item(BEFORE, 15, "U")
                multiply(0, 0)
                with eng.Fori(0, TURNS) as s:
                    turn(s, s, NQ)
                turn(AFTER, TURNS, QR)

                b = BLOCKS - 1
                act_low(0, b)
                turn_item(AFTER, 8, "D0", QR)
                turn_item(AFTER, 9, "D1", QR)
                turn_ad(b, QR)
                turn_item(AFTER, 10, "Bd0")
                turn_item(AFTER, 11, "Bd1")
                multiply(1, b)
                act_low(1, b)
                turn_item(AFTER, AL, "Al")
                turn_item(AFTER, 13, "scale")
                turn_item(AFTER, 14, "O")
                turn_item(AFTER, 15, "O")
                eng.wait_ge(down_added, START + h * DOWNS + b * ADDS)
                add_down(b, 0)
                eng.wait_ge(down_added, START + h * DOWNS + (b * ADDS + 1))
                t_sum(acc[0:Q, KT, :], 1, 2, pick_half)
                t_low(1, 2)
                for i in range(1, ADDS):
                    add_down(b, i)
                turn_item(AFTER, 16, "Bl0")
                item_full(eng, h, AFTER, 13)
                t_sum(ps[3][0:Q, :], 0, 3, pick_scale)
                turn_item(AFTER, 17, "Bl1")
                t_low(0, 3)
                turn_item(AFTER, 18, "O")
                turn_item(AFTER, 19, "O")
                eng.wait_ge(bias_loaded, NQ * 16)
                for k in range(KT):
                    if k + 4 < KT:
                        turn_item(AFTER, 20 + k, "O")
                    eng.wait_ge(out_done, START + h * KT + k + 1)
                    nc.vector.scalar_tensor_tensor(out=acc[:, k, :], in0=ps[k % 4][:, :], scalar=bias[:, k:k + 1],
                                                   in1=acc[:, k, :], op0=ALU.add, op1=ALU.add
                                                   ).then_inc(out_added, 1)
                    if k % 2:
                        eng.wait_ge(out_added, START + h * KT + k + 1)
                        for m in range(2):
                            eng.wait_ge(out_stored[m], START + h * (KT // 2 * NQ * 16) + k // 2 * (NQ * 16))
                            nc.vector.transpose(
                                stage[m][:, :, :].rearrange("p t (k i) -> p t k i", k=2),
                                acc[:, k - 1:k + 1, m * TT:(m + 1) * TT].rearrange("p k (t i) -> p t k i", i=Q)
                            ).then_inc(out_turned, 1)

        @block.tensor
        def _(eng):
            for sem_ in (*wk_used[0], *wk_used[1], *unit_done[0], *unit_done[1], down_done, out_done):
                eng.sem_inc(sem_, START)
            with eng.Fori(0, HALVES) as h:
                def matmul(dst, stationary, moving, start=False, stop=False):
                    return nc.tensor.matmul(dst, stationary, moving, start=start, stop=stop)

                def tok(p):
                    return slice(p * TT, (p + 1) * TT)

                def three(dst, w_hi, w_lo, moving, start, stop=False):
                    for p in range(NT):
                        matmul(dst[:, tok(p)], w_hi, moving[0][:, tok(p)], start=start)
                    for p in range(NT):
                        matmul(dst[:, tok(p)], w_hi, moving[1][:, tok(p)])
                    for p in range(NT):
                        last = matmul(dst[:, tok(p)], w_lo, moving[0][:, tok(p)], stop=stop)
                    return last

                def over_width(dst, j, m, item, stop=False):
                    for k in range(KT):
                        if k % 4 == 0:
                            item_full(eng, h, *item, granules=k // 4 + 1)
                        if item[0] is AFTER and item[1] >= AL:
                            eng.wait_ge(x1_full, h * KT + (k + 1))
                        last = three(dst, Wk[j][:, 0, k, 0:m], Wk[j][:, 1, k, 0:m],
                                     [X[:, 0, k, :], X[:, 1, k, :]], start=(k == 0), stop=(stop and k == KT - 1))
                        if k % 4 == 3:
                            last.then_inc(wk_used[j][k // 4], 1)

                def adapter(dst, stationary, moving):
                    for p in range(NT):
                        last = matmul(dst[:, tok(p)], stationary(p), moving[:, tok(p)], stop=True)
                    return last

                def units(c, b, m, items, b_items):
                    for w in range(2):
                        dst = ps[2 * c + w][0:m, :]
                        if c == 0:
                            eng.wait_ge(silu_done[0] if w == 0 else mult_done[0], START + h * BLOCKS + b)
                        else:
                            eng.wait_ge(down_added, START + h * DOWNS + b * ADDS)
                            eng.wait_ge(t_summed, h * T_CHAINS + 2)
                        over_width(dst, w, m, items[w])
                        item_full(eng, h, *b_items[w], granules=c + 1)
                        eng.wait_ge(t_full, h * T_CHAINS + w + 1)
                        adapter(dst, lambda p: Bf[:, w, c, p, 0:m], Tm[w]).then_inc(unit_done[w][c], 1)

                def down_tile(b, i, m, stop=True):
                    dst = ps[down_pair(b, i)]
                    for c in range(2):
                        if i == 0:
                            for p in range(NT):
                                stationary = Ad[0:m, c, p, :, :].rearrange("p l r -> p (l r)")
                                for l in range(2):
                                    last = matmul(dst[0:2 * Q, tok(p)], stationary, act[0:m, c, l, tok(p)],
                                                  start=(c == 0 and l == 0), stop=(c == 1 and l == 1))
                        else:
                            last = three(dst, Wd[0:m, c, 0, i - 1, :], Wd[0:m, c, 1, i - 1, :],
                                         [act[0:m, c, 0, :], act[0:m, c, 1, :]], start=(c == 0),
                                         stop=(stop and c == 1))
                    return last

                def down_operands(s, b, first):
                    for c in range(2):
                        eng.wait_ge(act_full[c], START + h * BLOCKS + b + 1)
                    eng.wait_ge(ad_full, START + h * BLOCKS + b + 1)
                    item_full(eng, h, s, first)
                    item_full(eng, h, s, first + 1)

                def turn(s, b, m):
                    units(1, b, P, [(s, -2), (s, -1)], [(s, -5), (s, -3)])
                    units(0, b + 1, m, [(s, 2), (s, 4)], [(s, 3), (s, 5)])
                    down_operands(s, b, 0)
                    base = h * DOWNS + b * ADDS
                    for i in range(ADDS):
                        if i < 2:
                            eng.wait_ge((silu_done, mult_done)[i][1], START + h * BLOCKS + b + 1)
                        else:
                            eng.wait_ge(down_added, START + base + (i - 1))
                        down_tile(b, i, P).then_inc(down_done, 1)

                eng.wait_ge(out_added, START + h * KT)
                for kq in range(2):
                    for p in range(NT):
                        item_full(eng, h, BEFORE, AGU[p], granules=kq + 1)
                        for n in X_AT[4 * kq + 2 * p:4 * kq + 2 * p + 2]:
                            item_full(eng, h, BEFORE, n)
                        for k in range(4 * kq, 4 * kq + 4):
                            for l in range(2):
                                last = matmul(ps[2][:, tok(p)], Wk[p][:, 0, k, :], X[:, l, k, tok(p)],
                                              start=(k == 0 and l == 0), stop=(k == KT - 1 and l == 1))
                        last.then_inc(wk_used[p][kq], 1)
                units(0, 0, P, [(BEFORE, 10), (BEFORE, 12)], [(BEFORE, 11), (BEFORE, 13)])
                with eng.Fori(0, TURNS) as s:
                    turn(s, s, P)
                turn(AFTER, TURNS, MR)

                b = BLOCKS - 1
                units(1, b, MR, [(AFTER, 6), (AFTER, 7)], [(AFTER, 3), (AFTER, 5)])
                down_operands(AFTER, b, 8)
                base = h * DOWNS + b * ADDS
                eng.wait_ge(silu_done[1], START + h * BLOCKS + BLOCKS)
                down_tile(b, 0, MR).then_inc(down_done, 1)
                for k in range(KT + 2):
                    if k < KT:
                        if k == 0:
                            eng.wait_ge(mult_done[1], START + h * BLOCKS + BLOCKS)
                        elif k == 1:
                            eng.wait_ge(silu_done[0], START + h * BLOCKS + BLOCKS)
                        elif k == 2:
                            eng.wait_ge(mult_done[0], START + h * BLOCKS + BLOCKS)
                        else:
                            eng.wait_ge(down_added, START + base + (k - 2))
                        down_tile(b, k + 1, MR, stop=False)
                    if k >= 2:
                        if k == 2:
                            eng.wait_ge(t_full, h * T_CHAINS + 3)
                            item_full(eng, h, AFTER, 10)
                            item_full(eng, h, AFTER, 11)
                        adapter(ps[down_pair(b, k - 1)], lambda p: Wk[0][0:3 * Q, p, k - 2, :], Tm[1]
                                ).then_inc(down_done, 1)

                eng.wait_ge(down_added, START + base + 6)
                item_full(eng, h, AFTER, AL)
                for k in range(KT):
                    eng.wait_ge(x1_full, h * KT + (k + 1))
                    for p in range(NT):
                        for l in range(2):
                            last = matmul(ps[3][0:2 * Q, tok(p)], Wk[1][:, 0, k, p * 2 * Q:(p + 1) * 2 * Q],
                                          X[:, l, k, tok(p)], start=(k == 0 and l == 0),
                                          stop=(k == KT - 1 and l == 1))
                    if k % 4 == 3:
                        last.then_inc(wk_used[1][k // 4], 1)
                for k in range(KT + 2):
                    if k < KT:
                        if k < 3:
                            eng.wait_ge(down_added, START + base + (7 + k))
                        elif k == 3:
                            eng.wait_ge(t_summed, h * T_CHAINS + 4)
                        else:
                            eng.wait_ge(out_added, START + h * KT + (k - 3))
                        over_width(ps[k % 4], k % 2, P, (AFTER, 14 + k + (2 if k >= 2 else 0)))
                    if k >= 2:
                        if k == 2:
                            eng.wait_ge(t_full, h * T_CHAINS + 4)
                            item_full(eng, h, AFTER, 16)
                            item_full(eng, h, AFTER, 17)
                        adapter(ps[(k - 2) % 4], lambda p: Wd[0:3 * Q, 0, p, k - 2, :], Tm[0]
                                ).then_inc(out_done, 1)


_INS = ["x", "itok_B_2_6", "itok_B_1_7", "L0_cond_W_gate", "L0_cond_W_up", "L0_cond_W_down",
        "L0_cond_A_gate", "L0_cond_B_gate", "L0_cond_A_up", "L0_cond_B_up", "L0_cond_A_down", "L0_cond_B_down",
        "L1_cond_weight", "L1_cond_bias", "L1_cond_lora_a_weights", "L1_cond_lora_b_weights",
        "L1_cond_scaling_factors"]
_OUTS = [((8, 256, 1024), "float32")]


def kernel(**inputs):
    import numpy as _np
    import concourse.bacc as _bacc
    from concourse import mybir as _mybir
    from concourse.bass_utils import run_bass_kernel_spmd as _run

    nc = _bacc.Bacc("TRN2", target_bir_lowering=False, num_devices=1)
    arrays, args = {}, []
    for name in _INS:
        a = _np.ascontiguousarray(inputs[name])
        arrays[f"in_{name}_dram"] = a
        args.append(nc.dram_tensor(f"in_{name}_dram", a.shape, _mybir.dt.from_np(a.dtype), kind="ExternalInput").ap())
    for i, (shape, dtype) in enumerate(_OUTS):
        dt = _mybir.dt.from_np(_np.dtype(dtype))
        args.append(nc.dram_tensor(f"out_{i}_dram", shape, dt, kind="ExternalOutput").ap())
    build(nc, *args)
    r = _run(nc, [arrays], core_ids=[0])
    return r.results[0]["out_0_dram"]
```

```python
from contextlib import ExitStack

import concourse.bass as bass
from concourse import mybir

F32 = mybir.dt.float32
F32R = mybir.dt.float32r
ACT = mybir.ActivationFunctionType
ALU = mybir.AluOpType

P = 128
Q = 32
NQ = P // Q
RAW = 4
TURNED = 2
START = 2
BEFORE, AFTER = "before", "after"


class Tally:

    def __init__(self, before, body, after, turns):
        self.before, self.body, self.turns = before, body, turns
        self.total = before + turns * body + after

    def at(self, h, s, n):
        if s is BEFORE:
            return h * self.total + n
        if s is AFTER:
            return h * self.total + (self.before + self.turns * self.body + n)
        return h * self.total + s * self.body + (self.before + n)


def build(nc, x, l0_index, l1_index, w_gate, w_up, w_down, a_gate, b_gate, a_up, b_up, a_down, b_down,
          w_out, bias_in, a_out, b_out, scale_in, out):
    NB, NS, H = x.shape
    F = w_gate.shape[0]
    R = a_gate.shape[2]
    HALVES = 2
    BH = NB // HALVES
    T = BH * NS
    TT = 512
    NT = T // TT
    KT = H // P
    HQ = H // NQ
    FB = 256
    TURNS = F // FB - 1
    HC = P // 2
    ADDS = KT + 1
    assert (NS, TT, 2 * R, F % FB, F // FB) == (256, 2 * NS, Q, P + HC, 10)
    assert l0_index.shape[0] == NB and NT == 2 and KT == 8

    tokens = x.rearrange("b s h -> (b s) h")
    out_tokens = out.rearrange("b s h -> (b s) h")

    with ExitStack() as ctx:
        def sbuf(name, shape, dtype=F32):
            return ctx.enter_context(nc.sbuf_tensor(name, shape, dtype))

        def sem(name):
            return ctx.enter_context(nc.semaphore(name))

        X = sbuf("X", [P, 2, KT, T], F32R)
        acc = sbuf("acc", [P, ADDS, T])
        act = sbuf("act", [P, 2, 2, T], F32R)
        Wd = sbuf("Wd", [P, 2, 2, KT, P], F32R)
        Wk = [sbuf(f"Wk{j}", [P, 2, KT, P], F32R) for j in range(2)]
        raw = [sbuf(f"raw{j}", [P, 1024]) for j in range(RAW)]
        turned = [sbuf(f"turned{j}", [P, 1024]) for j in range(TURNED)]
        work = [sbuf(f"work{j}", [P, T]) for j in range(2)]
        Bf = sbuf("Bf", [96, 2, 2, 2, P], F32R)
        Ad_raw = sbuf("Ad_raw", [2 * Q, FB])
        Ad_turned = sbuf("Ad_turned", [P, 2, 2, Q])
        Ad = sbuf("Ad", [P, 2, 2, 2, Q], F32R)
        Tm = [sbuf(f"Tm{j}", [96, T], F32R) for j in range(2)]
        stage = [sbuf(f"stage{j}", [P, 16, 64]) for j in range(2)]
        zeros = sbuf("zeros", [96, 2, HC])
        bias = sbuf("bias", [P, KT])
        scale_row = sbuf("scale_row", [Q, BH])
        pick = sbuf("pick", [Q, BH])
        pick_half = sbuf("pick_half", [Q, BH])
        pick_scale = sbuf("pick_scale", [Q, BH])

        ps = [ctx.enter_context(nc.psum_tensor(f"ps{j}", [P, T], F32)) for j in range(4)]

        raw_full = [sem(f"raw_full{j}") for j in range(RAW)]
        turned_full = [sem(f"turned_full{j}") for j in range(TURNED)]
        hi_full = [sem(f"hi_full{j}") for j in range(TURNED)]
        lo_full = [sem(f"lo_full{j}") for j in range(TURNED)]
        wk_used = [[sem(f"wk_used{j}{g}") for g in range(2)] for j in range(2)]
        ad_loaded, ad_turned, ad_hi, ad_full = (sem(n) for n in ("ad_loaded", "ad_turned", "ad_hi", "ad_full"))
        unit_done = [[sem(f"unit_done{w}{c}") for c in range(2)] for w in range(2)]
        silu_done = [sem(f"silu_done{c}") for c in range(2)]
        mult_done = [sem(f"mult_done{c}") for c in range(2)]
        act_hi = [sem(f"act_hi{c}") for c in range(2)]
        act_full = [sem(f"act_full{c}") for c in range(2)]
        t_copied, t_summed, t_masked, t_hi, t_full = (sem(n) for n in (
            "t_copied", "t_summed", "t_masked", "t_hi", "t_full"))
        down_done, down_added = sem("down_done"), sem("down_added")
        a_products = sem("a_products")
        down_t = sem("down_t")
        acc_set, x1_hi = sem("acc_set"), sem("x1_hi")
        x1_full = [sem(f"x1_full{j}") for j in range(2)]
        out_done, out_added, out_turned = (sem(n) for n in ("out_done", "out_added", "out_turned"))
        out_stored = [sem(f"out_stored{m}") for m in range(2)]
        bias_loaded, pick_set, pick_ready, zeros_set = (sem(n) for n in (
            "bias_loaded", "pick_set", "pick_ready", "zeros_set"))

        BLOCKS = TURNS + 2
        ITEMS_BEFORE, TURN_ITEMS, ITEMS_AFTER = 16, 8, 24
        FIRST_ITEMS = ["G", "x0", "x1", "U", "Agu0", "x2", "x3", "Agu1", "x4", "x5", "x6", "Bg", "x7", "Bu"]
        X_AT = [FIRST_ITEMS.index(f"x{i}") for i in range(8)]
        AGU = [FIRST_ITEMS.index(f"Agu{p}") for p in range(NT)]
        AL = 12
        DMAS = 4
        CHUNKS = [2 * BLOCKS, 2 * BLOCKS - 1]
        WK_USED = [CHUNKS[0] + KT // 2, CHUNKS[1] + 1 + KT // 2]
        DOWNS = BLOCKS * ADDS
        A_PRODUCTS = NT + 1
        T_PARTS = 4 * NT
        GATE_T, UP_T, DOWN_T, OUT_T = ([2 * p + w + 1 for p in range(NT)] if w < 2 else
                                       [2 * w + p + 1 for p in range(NT)] for w in range(4))

        def in_ring(ring, h, s, n):
            return n % ring, Tally(ITEMS_BEFORE // ring, TURN_ITEMS // ring, ITEMS_AFTER // ring, TURNS).at(
                h, s, n // ring)

        def turned_at(h, s, n):
            return in_ring(TURNED, h, s, n)

        def by_vector(n, item):
            return item[0] == "x" and int(item[1]) % 2 == 0

        def item_full(eng, h, s, n, granules=2):
            j, before = turned_at(h, s, n)
            eng.wait_ge(lo_full[j], START + before * 2 + granules)

        def down_pair(b, i):
            if isinstance(b, int) and b == BLOCKS - 1:
                return (3 + i) % 4
            return 3 - i % 2

        def out_pair(k):
            return (k + 1) % 4

        block = ctx.enter_context(nc.Block())

        @block.sync
        def _(sp):
            with sp.Fori(0, HALVES) as h:
                def indices(table, rows):
                    flat = table.rearrange("(o n) -> o n", o=1)
                    return [sp.value_load(flat[:, bass.ds(h * BH + b, 1)], min_val=0, max_val=rows - 1)
                            for b in range(BH)]

                def slot(s, n):
                    last = n - RAW
                    if s is BEFORE and last < 0:
                        for j in range(TURNED):
                            sp.wait_ge(turned_full[j], START + turned_at(h, BEFORE, 0)[1])
                    else:
                        j, before = turned_at(h, s, last)
                        sp.wait_ge(turned_full[j], START + before + 1)
                    return raw[n % RAW], raw_full[n % RAW]

                def load_rows(s, n, w, group, step, nq):
                    buf, full = slot(s, n)
                    rows = w.rearrange("(g i) m -> i g m", i=Q)
                    for c in range(NQ):
                        sp.dma_start(buf[c * Q:(c + 1) * Q, 0:nq * HQ].rearrange("i (q m) -> i q m", q=nq),
                                     rows[:, bass.ds(group, nq, step), c * HQ:(c + 1) * HQ]).then_inc(full, 16)

                def load_down(s, n, e, b):
                    buf, full = slot(s, n)
                    rows = w_down.rearrange("(g i) f -> i g f", i=Q)
                    for q in range(NQ):
                        sp.dma_start(buf[q * Q:(q + 1) * Q, :].rearrange("i (g f) -> i g f", f=2 * Q),
                                     rows[:, 16 * e:16 * e + 16, bass.ds(b * FB + q * 2 * Q, 2 * Q)]
                                     ).then_inc(full, 16)

                def load_last_down(n, c):
                    buf, full = slot(AFTER, n)
                    rows = w_down.rearrange("(g i) f -> i g f", i=Q)
                    for q in range(NQ):
                        first = (BLOCKS - 1) * FB + c * P + (q % 2 if c else q) * Q
                        sp.dma_start(buf[q * Q:(q + 1) * Q, :].rearrange("i (g f) -> i g f", f=Q),
                                     rows[:, :, first:first + Q]).then_inc(full, 16)

                def load_b(s, n, b_all, f0, each):
                    buf, full = slot(s, n)
                    for b in range(BH):
                        src = b_all[0, bass.ds(l0[b], 1), bass.ds(f0, Q * each), :]
                        sp.dma_start(buf[0:Q, b * 128:b * 128 + each * R],
                                     src.rearrange("o (i j) r -> (o i) (j r)", i=Q)).then_inc(full, 16)

                def load_b_pair(s, n, b_all, index, p):
                    buf, full = slot(s, n)
                    for b in range(2):
                        src = b_all[bass.ds(index[2 * p + b], 1), :, :].rearrange("o (i j) r -> (o i) (j r)", i=Q)
                        for m in range(2):
                            sp.dma_start(buf[0:Q, b * 512 + m * 256:b * 512 + (m + 1) * 256],
                                         src[:, m * 256:(m + 1) * 256]).then_inc(full, 16)

                def load_a(s, n, parts):
                    buf, full = slot(s, n)
                    for g, (a_all, index) in enumerate(parts):
                        sp.dma_start(buf[g * R:(g + 1) * R, :],
                                     a_all[bass.ds(index, 1), :, :].rearrange("o r m -> (o r) m")
                                     ).then_inc(full, 16)

                def load_ad(b, features):
                    for i in range(BH):
                        src = a_down[0, bass.ds(l0[i], 1), :, bass.ds(b * FB, features)]
                        sp.dma_start(Ad_raw[i * R:(i + 1) * R, 0:features],
                                     src.rearrange("o r m -> (o r) m")).then_inc(ad_loaded, 16)

                def load_turn(s, b, last=False):
                    load_down(s, 0, 0, b)
                    load_down(s, 1, 1, b)
                    sp.wait_ge(ad_turned, START + h * BLOCKS + b)
                    load_ad(b, FB)
                    first = (b + 1) * (FB // Q)
                    second, step, nq, each = (first + 4, 1, 2, 6) if last else (first + 1, 2, NQ, 8)
                    load_rows(s, 2, w_gate, first, step, NQ)
                    load_b(s, 3, b_gate, (b + 1) * FB, each)
                    load_rows(s, 4, w_up, first, step, NQ)
                    load_b(s, 5, b_up, (b + 1) * FB, each)
                    load_rows(s, 6, w_gate, second, step, nq)
                    load_rows(s, 7, w_up, second, step, nq)

                def load_x(n):
                    first_col, first_token = n // 4 * 128, n % 4 * 256
                    buf, full = slot(BEFORE, X_AT[n])
                    for c in range(NQ):
                        col = c * HQ + first_col
                        src = tokens[bass.ds(h * T + first_token, 256), col:col + 128]
                        sp.dma_start(buf[c * Q:(c + 1) * Q, :].rearrange("i (t m) -> i t m", t=8),
                                     src.rearrange("(t i) m -> i t m", i=Q)).then_inc(full, 16)

                def load_agu(p):
                    load_a(BEFORE, AGU[p], [(a, l0[2 * p + b]) for a in (a_gate[0], a_up[0]) for b in range(2)])

                load_rows(BEFORE, 0, w_gate, 0, 2, NQ)
                load_x(0)
                load_x(1)
                load_rows(BEFORE, 3, w_up, 0, 2, NQ)
                l0 = indices(l0_index, a_gate.shape[1])
                load_agu(0)
                load_x(2)
                load_x(3)
                load_agu(1)
                load_x(4)
                load_x(5)
                load_x(6)
                load_b(BEFORE, 11, b_gate, 0, 8)
                load_x(7)
                load_b(BEFORE, 13, b_up, 0, 8)
                load_rows(BEFORE, 14, w_gate, 1, 2, NQ)
                load_rows(BEFORE, 15, w_up, 1, 2, NQ)
                with sp.Fori(0, TURNS) as s:
                    load_turn(s, s)
                load_turn(AFTER, TURNS, last=True)
                l1 = indices(l1_index, a_out.shape[0])
                load_last_down(8, 0)
                load_last_down(9, 1)
                load_b_pair(AFTER, 10, b_down[0], l0, 0)
                load_b_pair(AFTER, 11, b_down[0], l0, 1)
                load_a(AFTER, AL, [(a_out, l1[b]) for b in range(BH)])
                sp.wait_ge(ad_turned, START + h * BLOCKS + (BLOCKS - 1))
                buf, full = slot(AFTER, 13)
                load_ad(BLOCKS - 1, P + HC)
                for b in range(BH):
                    factor = scale_in.rearrange("(n o) -> n o", o=1)[bass.ds(l1[b], 1), :]
                    sp.dma_start(buf[0:Q, b:b + 1], factor.to_broadcast([Q, 1]),
                                 allow_slow_non_contiguous=True).then_inc(full, 16)
                for k in range(KT):
                    if k == 2:
                        load_b_pair(AFTER, 16, b_out, l1, 0)
                        load_b_pair(AFTER, 17, b_out, l1, 1)
                    load_rows(AFTER, 14 + k + (2 if k >= 2 else 0), w_out, k, KT, NQ)

        def places(item, g, j, last=False, k_out=0):
            src, ks = turned[j], slice(4 * g, 4 * g + 4)
            if item in ("G", "U", "O"):
                wk = Wk[{"G": 0, "U": 1, "O": k_out % 2}[item]]
                return (src[:, :].rearrange("p (k m) -> p k m", k=KT)[:, ks, :],
                        [wk[:, 0, ks, :]], wk[:, 1, ks, :])
            if item in ("Gh", "Uh"):
                cols = slice(0, HC) if item == "Gh" else slice(HC, P)
                return (src[:, 0:KT * HC].rearrange("p (k m) -> p k m", k=KT)[:, ks, :],
                        [Wk[0][:, 0, ks, cols]], Wk[0][:, 1, ks, cols])
            if item in ("Agu0", "Agu1", "Al"):
                home = (Wk[1][:, 0] if item == "Al" else Wd[:, 1, int(item[3])])[:, ks, :]
                home = home.rearrange("p k (w l r) -> p k w l r", w=2, l=2)
                return (src[:, 0:512].rearrange("p (k w r) -> p k w r", k=KT, w=2)[:, ks, :, :],
                        [home[:, :, :, 0, :]], home[:, :, :, 1, :])
            if item[0] == "D":
                c, e = (int(item[2]), g) if item[1] == "c" else (g, int(item[1]))
                hi_lo = [Wd[:, c, l, :, e * 64:(e + 1) * 64].rearrange("p k (q i) -> p q k i", q=2)
                         for l in range(2)]
                return (src[:, g * 512:(g + 1) * 512].rearrange("p (q k i) -> p q k i", q=2, k=KT),
                        [hi_lo[0]], hi_lo[1])
            if item in ("Bg", "Bu"):
                w = "gu".index(item[1])
                cols = slice(w * HC, (w + 1) * HC) if last and g else slice(0, P)
                rows = [Bf[r * Q:(r + 1) * Q, w, g, :, cols].rearrange("p w (q i) -> p w q i", i=Q)
                        for r in range(3)]
                src = src[0:Q, 0:2 * FB]
                if last:
                    src = src.rearrange("p (w q i) -> p w q i", w=2, i=Q)[:, :, 4 * g:4 * g + (2 if g else 4), :]
                else:
                    src = src.rearrange("p (w q c i) -> p w q c i", w=2, q=NQ, c=2)[:, :, :, g, :]
                return src, rows[0:2], rows[2]
            if item[0] == "x":
                n = int(item[1])
                ks, ts = slice(n // 4 * 4 + 2 * g, n // 4 * 4 + 2 * g + 2), slice(n % 4 * 256, n % 4 * 256 + 256)
                return (src[:, :].rearrange("p (k t) -> p k t", k=4)[:, 2 * g:2 * g + 2, :],
                        [X[:, 0, ks, ts]], X[:, 1, ks, ts])
            if item == "scale":
                return src[0:Q, 2 * g:2 * g + 2], [scale_row[:, 2 * g:2 * g + 2]], pick_scale[:, 2 * g:2 * g + 2]
            p = int(item[2])
            home = Wk[0][:, p] if item[1] == "d" else Wd[:, 0, p]
            rows = [home[r * Q:(r + 1) * Q, ks, :].rearrange("p k (q i) -> p q k i", q=NQ) for r in range(3)]
            return (src[0:Q, :].rearrange("p (q k i) -> p q k i", q=NQ, k=KT)[:, :, ks, :], rows[0:2], rows[2])

        @block.scalar
        def _(act_eng):
            eng = act_eng
            for sem_ in (*silu_done, *out_stored):
                eng.sem_inc(sem_, START)
            eng.wait_ge(zeros_set, 1)
            with eng.Fori(0, HALVES) as h:
                def home_free(item, g, n):
                    if item in ("Agu0", "Agu1"):
                        eng.wait_ge(down_done, START + h * DOWNS)
                    elif item[0] == "x":
                        eng.wait_ge(wk_used[1][int(item[1]) // 4], START + h * WK_USED[1])
                    elif item in ("G", "Gh", "Uh"):
                        eng.wait_ge(wk_used[0][g], START + h * WK_USED[0] + n)
                    elif item == "U":
                        eng.wait_ge(wk_used[1][g], START + h * WK_USED[1] + n)
                    elif item in ("Bg", "Bu"):
                        eng.wait_ge(unit_done["gu".index(item[1])][g], START + h * BLOCKS + n)
                    elif item[0] == "D":
                        eng.wait_ge(down_done, START + h * DOWNS + n * ADDS)
                        eng.wait_ge(a_products, h * A_PRODUCTS + NT)
                        eng.wait_ge(out_done, START + h * KT * NT)
                    elif item in ("Bd0", "Bd1"):
                        for gg in range(2):
                            eng.wait_ge(wk_used[0][gg], START + h * WK_USED[0] + CHUNKS[0])
                    elif item == "Al":
                        eng.wait_ge(wk_used[1][g], START + h * WK_USED[1] + CHUNKS[1])
                    elif item == "O":
                        eng.wait_ge(wk_used[n % 2][g], START + h * WK_USED[n % 2] + (CHUNKS[n % 2] + n % 2 + n // 2))
                        eng.wait_ge(down_done, START + h * DOWNS + DOWNS)
                    elif item in ("Bl0", "Bl1"):
                        eng.wait_ge(down_done, START + h * DOWNS + DOWNS)

                def hi(s, n, item, at=0, last_b=False):
                    j, before = turned_at(h, s, n)
                    eng.wait_ge(turned_full[j], START + before + 1)
                    for g in range(2):
                        home_free(item, g, at)
                        src, homes, _ = places(item, g, j, last_b, at)
                        if last_b and g:
                            w = "gu".index(item[1])
                            nc.scalar.activation(Bf[:, w, g, :, (1 - w) * HC:(2 - w) * HC], zeros[:, :, :], ACT.Copy)
                        for home in homes:
                            last = nc.scalar.activation(home, src, ACT.Copy)
                        last.then_inc(hi_full[j], 1)

                def silu(c, b, m=P):
                    eng.wait_ge(unit_done[0][c], START + h * BLOCKS + b + 1)
                    if m < P:
                        eng.wait_ge(unit_done[1][c], START + h * BLOCKS + b + 1)
                    eng.wait_ge(act_full[c], START + h * BLOCKS + b)
                    eng.wait_ge(t_full, h * T_PARTS + 2 * NT)
                    nc.scalar.activation(work[c][0:m, :], ps[2 * c][0:m, :], ACT.Silu).then_inc(silu_done[c], 1)

                def act_high(c, b, m=P):
                    eng.wait_ge(mult_done[c], START + h * BLOCKS + b + 1)
                    eng.wait_ge(down_done, START + h * DOWNS + b * ADDS)
                    nc.scalar.activation(act[0:m, c, 0, :], work[c][0:m, :], ACT.Copy).then_inc(act_hi[c], 1)

                def ad_high(b):
                    eng.wait_ge(ad_turned, START + h * BLOCKS + b + 1)
                    eng.wait_ge(down_done, START + h * DOWNS + b * ADDS)
                    nc.scalar.activation(Ad[:, :, :, 0, :], Ad_turned[:, :, :, :], ACT.Copy).then_inc(ad_hi, 1)

                def t_copy(src, w, p):
                    ts = slice(p * TT, (p + 1) * TT)
                    nc.scalar.activation(work[w][0:Q, ts], src[:, ts], ACT.Copy).then_inc(t_copied, 1)

                def t_high(w, p, part):
                    ts = slice(p * TT, (p + 1) * TT)
                    eng.wait_ge(t_masked, h * T_PARTS + part)
                    nc.scalar.activation(Tm[w][0:Q, ts], work[w][0:Q, ts], ACT.Copy)
                    nc.scalar.activation(Tm[w][2 * Q:3 * Q, ts], work[w][0:Q, ts], ACT.Copy).then_inc(t_hi, 1)

                def turn(s, b, last=False):
                    act_high(0, b)
                    hi(s, 0, "D0", b)
                    hi(s, 1, "D1", b)
                    ad_high(b)
                    hi(s, 2, "G", 2 * b + 2)
                    silu(1, b)
                    hi(s, 3, "Bg", b + 1, last)
                    hi(s, 4, "U", 2 * b + 2)
                    act_high(1, b)
                    hi(s, 5, "Bu", b + 1, last)
                    silu(0, b + 1)
                    hi(s, 6, "Gh" if last else "G", 2 * b + 3)
                    hi(s, 7, "Uh" if last else "U", 2 * b + 3)

                for n, item in enumerate(FIRST_ITEMS):
                    hi(BEFORE, n, item)
                for p in range(NT):
                    eng.wait_ge(a_products, h * A_PRODUCTS + (p + 1))
                    t_copy(ps[2][Q:2 * Q, :], 0, p)
                    t_copy(ps[2][3 * Q:4 * Q, :], 1, p)
                for p in range(NT):
                    t_high(0, p, GATE_T[p])
                    t_high(1, p, UP_T[p])
                silu(0, 0)
                hi(BEFORE, 14, "G", 1)
                hi(BEFORE, 15, "U", 1)
                with eng.Fori(0, TURNS) as s:
                    turn(s, s)
                turn(AFTER, TURNS, last=True)

                act_high(0, BLOCKS - 1)
                hi(AFTER, 8, "Dc0", BLOCKS - 1)
                hi(AFTER, 9, "Dc1", BLOCKS - 1)
                ad_high(BLOCKS - 1)
                silu(1, BLOCKS - 1, HC)
                hi(AFTER, 10, "Bd0")
                hi(AFTER, 11, "Bd1")
                act_high(1, BLOCKS - 1, HC)
                eng.wait_ge(act_full[1], START + h * BLOCKS + BLOCKS)
                eng.wait_ge(down_t, h + 1)
                t_copy(acc[Q:2 * Q, KT, :], 1, 0)
                eng.wait_ge(down_added, START + h * DOWNS + ((BLOCKS - 1) * ADDS + 1))
                t_copy(acc[Q:2 * Q, KT, :], 1, 1)
                for p in range(NT):
                    t_high(1, p, DOWN_T[p])
                for k in range(KT):
                    if k == 1:
                        hi(AFTER, AL, "Al")
                    elif k == 2:
                        hi(AFTER, 13, "scale")
                    eng.wait_ge(down_added, START + h * DOWNS + (BLOCKS - 1) * ADDS + 2 + k)
                    nc.scalar.activation(X[:, 0, k, :], acc[:, k, :], ACT.Copy).then_inc(x1_hi, 1)
                hi(AFTER, 14, "O", 0)
                eng.wait_ge(a_products, h * A_PRODUCTS + NT + 1)
                t_copy(ps[0][Q:2 * Q, :], 0, 0)
                eng.wait_ge(wk_used[1][1], START + h * WK_USED[1] + (CHUNKS[1] + 1))
                t_copy(ps[0][Q:2 * Q, :], 0, 1)
                hi(AFTER, 15, "O", 1)
                hi(AFTER, 16, "Bl0")
                for p in range(NT):
                    t_high(0, p, OUT_T[p])
                hi(AFTER, 17, "Bl1")

                def store(pair):
                    for m in range(2):
                        eng.wait_ge(out_turned, START + h * KT + (2 * pair + m + 1))
                        for q in range(NQ):
                            col = q * HQ + pair * 2 * Q
                            rows = out_tokens[bass.ds(h * T + m * TT, TT), col:col + 2 * Q]
                            eng.dma_start(rows.rearrange("(t i) m -> i t m", i=Q),
                                          stage[m][q * Q:(q + 1) * Q, :, :]).then_inc(out_stored[m], 16)

                for k in range(KT):
                    if k + 2 < KT:
                        hi(AFTER, 18 + k, "O", k + 2)
                    if k % 2:
                        store(k // 2)
            for m in range(2):
                eng.wait_ge(out_stored[m], START + HALVES * (KT // 2) * NQ * 16)

        @block.gpsimd
        def _(eng):
            for sem_ in (*lo_full, ad_full):
                eng.sem_inc(sem_, START)
            for q in range(NQ):
                eng.dma_start(bias[q * Q:(q + 1) * Q, :],
                              bias_in.rearrange("(q k i) -> q i k", q=NQ, k=KT)[q],
                              allow_slow_non_contiguous=True).then_inc(bias_loaded, 16)
            eng.memset(zeros[:, :, :], 0.0).then_inc(zeros_set, 1)
            eng.memset(pick[:, :], 1.0).then_inc(pick_set, 1)
            eng.wait_ge(pick_set, 1)
            parity = pick[:, :].rearrange("p (w b) -> p w b", b=2)
            eng.affine_select(out=parity[:, :, 0], in_=parity[:, :, 0], compare_op=ALU.is_ge, fill=0.0,
                              base=R - 1, pattern=[[0, 2]], channel_multiplier=-1).then_inc(pick_set, 1)
            eng.affine_select(out=parity[:, :, 1], in_=parity[:, :, 1], compare_op=ALU.is_ge, fill=0.0,
                              base=-R, pattern=[[0, 2]], channel_multiplier=1).then_inc(pick_set, 1)
            eng.wait_ge(pick_set, 3)
            nc.gpsimd.tensor_scalar(pick_half[:, :], pick[:, :], 0.5, None, ALU.mult).then_inc(pick_ready, 1)
            with eng.Fori(0, HALVES) as h:
                def lo(s, n, item, at=0, last_b=False):
                    j, before = turned_at(h, s, n)
                    across = item[0] == "B"
                    if across:
                        item_full(eng, h, s, n - 1)
                        if item == "Bd0":
                            eng.wait_ge(ad_full, START + h * BLOCKS + BLOCKS)
                    for g in range(2):
                        eng.wait_ge(hi_full[j], before * 2 + (g + 1))
                        src, homes, home = places(item, g, j, last_b, at)
                        if item == "scale":
                            nc.gpsimd.tensor_tensor(home, homes[0], pick[:, 2 * g:2 * g + 2],
                                                    ALU.mult).then_inc(lo_full[j], 1)
                        else:
                            nc.gpsimd.tensor_tensor(home, src, homes[0].bitcast(F32),
                                                    ALU.subtract).then_inc(lo_full[j], 1)
                        if across:
                            item_full(eng, h, s, n, granules=g + 1)

                def ad_low(b):
                    eng.wait_ge(ad_hi, h * BLOCKS + b + 1)
                    nc.gpsimd.tensor_tensor(Ad[:, :, :, 1, :], Ad_turned[:, :, :, :],
                                            Ad[:, :, :, 0, :].bitcast(F32), ALU.subtract).then_inc(ad_full, 1)

                def x1_low(k):
                    eng.wait_ge(x1_hi, h * KT + k + 1)
                    nc.gpsimd.tensor_tensor(X[:, 1, k, :], acc[:, k, :], X[:, 0, k, :].bitcast(F32),
                                            ALU.subtract).then_inc(x1_full[0], 1)

                def acc_start(ks):
                    for k in ks:
                        nc.gpsimd.tensor_tensor(acc[:, k, :], X[:, 0, k, :].bitcast(F32),
                                                X[:, 1, k, :].bitcast(F32), ALU.add).then_inc(acc_set, 1)

                def turn(s, b, last=False):
                    lo(s, 0, "D0")
                    lo(s, 1, "D1")
                    ad_low(b)
                    for n, item in enumerate(("G", "Bg", "U", "Bu", "Gh" if last else "G", "Uh" if last else "U")):
                        lo(s, 2 + n, item, last_b=last)

                for n, item in enumerate(FIRST_ITEMS):
                    if not by_vector(n, item):
                        lo(BEFORE, n, item)
                eng.wait_ge(out_turned, START + h * KT)
                for n in X_AT:
                    item_full(eng, h, BEFORE, n)
                acc_start(range(0, 4))
                lo(BEFORE, 14, "G")
                acc_start(range(4, 6))
                lo(BEFORE, 15, "U")
                acc_start(range(6, 8))
                with eng.Fori(0, TURNS) as s:
                    turn(s, s)
                turn(AFTER, TURNS, last=True)
                lo(AFTER, 8, "Dc0")
                lo(AFTER, 9, "Dc1")
                ad_low(BLOCKS - 1)
                lo(AFTER, 10, "Bd0")
                lo(AFTER, 11, "Bd1")
                x1_low(0)
                lo(AFTER, AL, "Al")
                lo(AFTER, 13, "scale")
                for k in range(2, KT, 2):
                    x1_low(k)
                lo(AFTER, 14, "O", 0)
                lo(AFTER, 15, "O", 1)
                lo(AFTER, 16, "Bl0")
                lo(AFTER, 17, "Bl1")
                for k in range(2, KT):
                    lo(AFTER, 16 + k, "O", k)

        @block.vector
        def _(eng):
            for sem_ in (*turned_full, ad_turned, *act_full, *mult_done, down_added, out_turned, out_added):
                eng.sem_inc(sem_, START)
            with eng.Fori(0, HALVES) as h:
                def turn_item(s, n, item, nq=NQ):
                    j, before = turned_at(h, s, n)
                    jr, loaded = in_ring(RAW, h, s, n)
                    eng.wait_ge(raw_full[jr], (loaded + 1) * (DMAS * 16))
                    eng.wait_ge(lo_full[j], START + before * 2)
                    src, dst = raw[jr], turned[j]
                    if item in ("G", "U", "Gh", "Uh", "O"):
                        last = nc.vector.transpose(
                            dst[:, 0:KT * nq * Q].rearrange("p (k q i) -> p k q i", k=KT, q=nq),
                            src[:, 0:nq * HQ].rearrange("p (q k i) -> p k q i", q=nq, k=KT))
                    elif item in ("Agu0", "Agu1", "Al"):
                        for w in range(2):
                            for q in range(NQ):
                                last = nc.vector.transpose(
                                    dst[q * Q:(q + 1) * Q, 0:512].rearrange(
                                        "p (k w i) -> p k w i", k=KT, w=2)[:, :, w, :],
                                    src[w * Q:(w + 1) * Q, q * HQ:(q + 1) * HQ].rearrange(
                                        "p (k i) -> p k i", k=KT))
                    elif item[0] == "x":
                        last = nc.vector.transpose(dst[:, :].rearrange("p (k t i) -> p k t i", k=4, t=8),
                                                   src[:, :].rearrange("p (t k i) -> p k t i", t=8, k=4))
                    elif item in ("Dc0", "Dc1"):
                        last = nc.vector.transpose(dst[:, :], src[:, :])
                    elif item in ("D0", "D1"):
                        last = nc.vector.transpose(
                            dst[:, :].rearrange("p (c g i) -> p c g i", c=2, g=16),
                            src[:, :].rearrange("p (g c i) -> p c g i", g=16, c=2))
                    elif item in ("Bg", "Bu"):
                        each = 2 * nq
                        for w in range(NT):
                            last = nc.vector.transpose(
                                dst[0:Q, w * FB:w * FB + Q * each].rearrange("p (i j) -> p j i", j=each),
                                src[0:Q, w * FB:(w + 1) * FB].rearrange("p (b j r) -> p j b r", b=2, r=R)[
                                    :, 0:each, :, :])
                    elif item == "scale":
                        last = nc.vector.tensor_copy(dst[0:Q, 0:BH], src[0:Q, 0:BH])
                    else:
                        last = nc.vector.transpose(
                            dst[0:Q, :].rearrange("p (i j) -> p j i", j=Q),
                            src[0:Q, :].rearrange("p (b j r) -> p j b r", b=2, r=R))
                    last.then_inc(turned_full[j], 1)

                def item_low(n, item):
                    j, before = turned_at(h, BEFORE, n)
                    for g in range(2):
                        eng.wait_ge(hi_full[j], before * 2 + (g + 1))
                        src, homes, home = places(item, g, j)
                        nc.vector.tensor_tensor(home, src, homes[0].bitcast(F32), ALU.subtract
                                                ).then_inc(lo_full[j], 1)

                def turn_ad(b, last=False):
                    eng.wait_ge(ad_loaded, (h * BLOCKS + b + 1) * BH * 16)
                    eng.wait_ge(ad_full, START + h * BLOCKS + b)
                    for w in range(NT):
                        for q in range(NQ):
                            groups = slice(q, q + 5 - q // 2 * 2, 4 - q // 2 * 2) if last else slice(2 * q, 2 * q + 2)
                            done = nc.vector.transpose(
                                Ad_turned[q * Q:(q + 1) * Q, :, w, :],
                                Ad_raw[w * Q:(w + 1) * Q, :].rearrange("p (z i) -> p z i", i=Q)[:, groups, :])
                    done.then_inc(ad_turned, 1)

                def multiply(c, b, up, m=P):
                    eng.wait_ge(unit_done[1][c], START + h * BLOCKS + b + 1)
                    eng.wait_ge(silu_done[c], START + h * BLOCKS + b + 1)
                    nc.vector.tensor_tensor(work[c][0:m, :], work[c][0:m, :], up, ALU.mult
                                            ).then_inc(mult_done[c], 1)

                def act_low(c, b):
                    eng.wait_ge(act_hi[c], h * BLOCKS + b + 1)
                    nc.vector.tensor_tensor(act[:, c, 1, :], work[c][:, :], act[:, c, 0, :].bitcast(F32),
                                            ALU.subtract).then_inc(act_full[c], 1)

                def t_sum(src, w, p, part, factors):
                    one = work[w][0:Q, p * TT:(p + 1) * TT]
                    eng.wait_ge(t_copied, h * T_PARTS + part)
                    nc.vector.tensor_tensor(one, one, src[:, p * TT:(p + 1) * TT], ALU.add).then_inc(t_summed, 1)
                    eng.wait_ge(t_summed, h * T_PARTS + part)
                    one = one.rearrange("p (b t) -> p b t", b=2)
                    nc.vector.tensor_tensor(one, one, factors[:, 2 * p:2 * p + 2].unsqueeze(2).to_broadcast([Q, 2, NS]),
                                            ALU.mult).then_inc(t_masked, 1)

                def t_low(w, p, part):
                    ts = slice(p * TT, (p + 1) * TT)
                    eng.wait_ge(t_hi, h * T_PARTS + part)
                    nc.vector.tensor_tensor(Tm[w][Q:2 * Q, ts], work[w][0:Q, ts], Tm[w][0:Q, ts].bitcast(F32),
                                            ALU.subtract).then_inc(t_full, 1)

                def x1_low(k):
                    eng.wait_ge(x1_hi, h * KT + k + 1)
                    nc.vector.tensor_tensor(X[:, 1, k, :], acc[:, k, :], X[:, 0, k, :].bitcast(F32),
                                            ALU.subtract).then_inc(x1_full[1], 1)

                def add_down(b, i):
                    base = h * DOWNS + b * ADDS
                    pair = down_pair(b, i)
                    eng.wait_ge(down_done, START + base + i + 1)
                    dst = acc[0:2 * Q, KT, :] if i == 0 else acc[:, i - 1, :]
                    src = ps[pair][0:2 * Q, :] if i == 0 else ps[pair][:, :]
                    nc.vector.tensor_tensor(dst, dst, src, ALU.add).then_inc(down_added, 1)

                def turn(s, b, last=False):
                    act_low(0, b)
                    turn_item(s, 0, "D0")
                    turn_item(s, 1, "D1")
                    turn_ad(b)
                    turn_item(s, 2, "G")
                    turn_item(s, 3, "Bg", 3 if last else NQ)
                    turn_item(s, 4, "U")
                    multiply(1, b, ps[3][:, :])
                    act_low(1, b)
                    turn_item(s, 5, "Bu", 3 if last else NQ)
                    turn_item(s, 6, "Gh" if last else "G", 2 if last else NQ)
                    turn_item(s, 7, "Uh" if last else "U", 2 if last else NQ)
                    multiply(0, b + 1, ps[1][:, :])
                    eng.wait_ge(down_added, START + h * DOWNS + b * ADDS)
                    eng.wait_ge(acc_set, h * (KT + 1) + (KT + 1))
                    for i in range(ADDS):
                        add_down(b, i)

                for n, item in enumerate(FIRST_ITEMS):
                    turn_item(BEFORE, n, item)
                    if n and by_vector(n - 1, FIRST_ITEMS[n - 1]):
                        item_low(n - 1, FIRST_ITEMS[n - 1])
                eng.wait_ge(pick_ready, 1)
                for p in range(NT):
                    t_sum(ps[2][0:Q, :], 0, p, GATE_T[p], pick_half)
                    t_sum(ps[2][2 * Q:3 * Q, :], 1, p, UP_T[p], pick_half)
                for p in range(NT):
                    t_low(0, p, GATE_T[p])
                    t_low(1, p, UP_T[p])
                turn_item(BEFORE, 14, "G")
                turn_item(BEFORE, 15, "U")
                nc.vector.memset(acc[0:2 * Q, KT, :], 0.0).then_inc(acc_set, 1)
                multiply(0, 0, ps[1][:, :])
                with eng.Fori(0, TURNS) as s:
                    turn(s, s)
                turn(AFTER, TURNS, last=True)

                b = BLOCKS - 1
                act_low(0, b)
                turn_item(AFTER, 8, "Dc0")
                turn_item(AFTER, 9, "Dc1")
                turn_ad(b, last=True)
                turn_item(AFTER, 10, "Bd0")
                turn_item(AFTER, 11, "Bd1")
                multiply(1, b, ps[2][HC:P, :], HC)
                eng.wait_ge(act_hi[1], h * BLOCKS + b + 1)
                nc.vector.tensor_tensor(act[HC:P, 1, 0, :], work[1][0:HC, :], act[0:HC, 1, 0, :].bitcast(F32),
                                        ALU.subtract).then_inc(act_full[1], 1)
                eng.wait_ge(down_added, START + h * DOWNS + b * ADDS)
                eng.wait_ge(down_done, START + h * DOWNS + b * ADDS + 1)
                for p in range(NT):
                    part = acc[0:2 * Q, KT, p * TT:(p + 1) * TT]
                    nc.vector.tensor_tensor(part, part, ps[down_pair(b, 0)][0:2 * Q, p * TT:(p + 1) * TT],
                                            ALU.add).then_inc((down_t, down_added)[p], 1)
                for p in range(NT):
                    t_sum(acc[0:Q, KT, :], 1, p, DOWN_T[p], pick_half)
                for p in range(NT):
                    t_low(1, p, DOWN_T[p])
                for k in range(KT):
                    add_down(b, k + 1)
                    if k % 2 == 0 and k > 0:
                        x1_low(k - 1)
                    if k < 4:
                        turn_item(AFTER, AL + k, ("Al", "scale", "O", "O")[k])
                x1_low(KT - 1)
                turn_item(AFTER, 16, "Bl0")
                item_full(eng, h, AFTER, 13)
                for p in range(NT):
                    t_sum(ps[0][0:Q, :], 0, p, OUT_T[p], pick_scale)
                turn_item(AFTER, 17, "Bl1")
                for p in range(NT):
                    t_low(0, p, OUT_T[p])
                turn_item(AFTER, 18, "O")
                turn_item(AFTER, 19, "O")
                eng.wait_ge(bias_loaded, NQ * 16)
                for k in range(KT):
                    if k + 4 < KT:
                        turn_item(AFTER, 20 + k, "O")
                    for p in range(NT):
                        ts, out_count = slice(p * TT, (p + 1) * TT), h * KT * NT + k * NT + p + 1
                        eng.wait_ge(out_done, START + out_count)
                        nc.vector.scalar_tensor_tensor(out=acc[:, k, ts], in0=ps[out_pair(k)][:, ts],
                                                       scalar=bias[:, k:k + 1], in1=acc[:, k, ts],
                                                       op0=ALU.add, op1=ALU.add).then_inc(out_added, 1)
                        if k % 2:
                            eng.wait_ge(out_added, START + out_count)
                            eng.wait_ge(out_stored[p], START + h * (KT // 2 * NQ * 16) + k // 2 * (NQ * 16))
                            nc.vector.transpose(
                                stage[p][:, :, :].rearrange("p t (k i) -> p t k i", k=2),
                                acc[:, k - 1:k + 1, ts].rearrange("p k (t i) -> p t k i", i=Q)
                            ).then_inc(out_turned, 1)

        @block.tensor
        def _(eng):
            for sem_ in (*wk_used[0], *wk_used[1], *unit_done[0], *unit_done[1], down_done, out_done):
                eng.sem_inc(sem_, START)
            with eng.Fori(0, HALVES) as h:
                def matmul(dst, stationary, moving, start=False, stop=False):
                    return nc.tensor.matmul(dst, stationary, moving, start=start, stop=stop)

                def tok(p):
                    return slice(p * TT, (p + 1) * TT)

                def three(dst, w_hi, w_lo, moving, start=False, stop=False, pairs=range(NT)):
                    for p in pairs:
                        matmul(dst[:, tok(p)], w_hi, moving[0][:, tok(p)], start=start)
                    for p in pairs:
                        matmul(dst[:, tok(p)], w_hi, moving[1][:, tok(p)])
                    for p in pairs:
                        last = matmul(dst[:, tok(p)], w_lo, moving[0][:, tok(p)], stop=stop)
                    return last

                def tiles(dst, j, ks, pairs=range(NT), stop=False):
                    for k in ks:
                        last = three(dst, Wk[j][:, 0, k, :], Wk[j][:, 1, k, :], [X[:, 0, k, :], X[:, 1, k, :]],
                                     start=(k == 0), stop=(stop and k == KT - 1), pairs=pairs)
                    return last

                def over_width(dst, j, items):
                    for g in range(2):
                        for item in items:
                            item_full(eng, h, *item, granules=g + 1)
                        tiles(dst, j, range(4 * g, 4 * g + 4)).then_inc(wk_used[j][g], 1)

                def adapter(dst, stationary, moving, p, stop=True):
                    return matmul(dst[:, tok(p)], stationary, moving[:, tok(p)], stop=stop)

                def adapters(dst, w, c, parts, stop=True):
                    for p in range(NT):
                        eng.wait_ge(t_full, h * T_PARTS + parts[p])
                        last = adapter(dst, Bf[:, w, c, p, :], Tm[w], p, stop)
                    last.then_inc(unit_done[w][c], 1)

                def units(c, b, items, b_items):
                    for w in range(2):
                        if c == 0:
                            eng.wait_ge(silu_done[0] if w == 0 else mult_done[0], START + h * BLOCKS + b)
                        else:
                            eng.wait_ge(down_added, START + h * DOWNS + b * ADDS - 1 + w)
                            eng.wait_ge(t_summed, h * T_PARTS + 2 * NT)
                        over_width(ps[2 * c + w], w, [items[w]])
                        item_full(eng, h, *b_items[w], granules=c + 1)
                        adapters(ps[2 * c + w], w, c, (GATE_T, UP_T)[w])

                def a_down(dst, c, half, stop):
                    for p in range(NT):
                        stationary = Ad[:, c, p, :, :].rearrange("p l r -> p (l r)")
                        parts = 1 if half else 2
                        for l in range(parts):
                            last = matmul(dst[0:2 * Q, tok(p)], stationary, act[:, c, l, tok(p)],
                                          start=(c == 0 and l == 0), stop=(stop and l == parts - 1))
                    return last

                def down_tile(dst, k, c, stop=False):
                    return three(dst, Wd[:, c, 0, k, :], Wd[:, c, 1, k, :], [act[:, c, 0, :], act[:, c, 1, :]],
                                 start=(c == 0), stop=stop)

                def down_tile_half(dst, k):
                    for p in range(NT):
                        matmul(dst[:, tok(p)], Wd[:, 1, 0, k, :], act[:, 1, 0, tok(p)])
                    for p in range(NT):
                        matmul(dst[:, tok(p)], Wd[0:HC, 1, 1, k, :], act[0:HC, 1, 0, tok(p)])

                def turn(s, b, last=False):
                    units(1, b, [(s, -2), (s, -1)], [(s, -5), (s, -3)])
                    units(0, b + 1, [(s, 2), (s, 4)], [(s, 3), (s, 5)])
                    for c in range(2):
                        eng.wait_ge(act_full[c], START + h * BLOCKS + b + 1)
                    eng.wait_ge(ad_full, START + h * BLOCKS + b + 1)
                    item_full(eng, h, s, 0)
                    item_full(eng, h, s, 1)
                    for i in range(ADDS):
                        dst = ps[down_pair(b, i)]
                        if i < 2:
                            eng.wait_ge((mult_done, silu_done)[i][1], START + h * BLOCKS + b + 1)
                        else:
                            eng.wait_ge(down_added, START + h * DOWNS + b * ADDS + (i - 1))
                        for c in range(2):
                            done = (a_down(dst, c, False, c == 1) if i == 0 else
                                    down_tile(dst, i - 1, c, stop=(c == 1)))
                        done.then_inc(down_done, 1)

                def a_gate_up(p, kq):
                    item_full(eng, h, BEFORE, AGU[p], granules=kq + 1)
                    for k in range(4 * kq, 4 * kq + 4):
                        for l in range(2):
                            last = matmul(ps[2][:, tok(p)], Wd[:, 1, p, k, :], X[:, l, k, tok(p)],
                                          start=(k == 0 and l == 0), stop=(k == KT - 1 and l == 1))
                    return last

                def x_loaded(p, kq):
                    for n in X_AT[4 * kq + 2 * p:4 * kq + 2 * p + 2]:
                        item_full(eng, h, BEFORE, n)

                def first_unit(w, p, kq):
                    item_full(eng, h, BEFORE, (0, 3)[w], granules=kq + 1)
                    return tiles(ps[w], w, range(4 * kq, 4 * kq + 4), pairs=[p])

                eng.wait_ge(out_added, START + h * KT * NT)
                for p in range(NT):
                    x_loaded(p, 0)
                    for w in range(2):
                        last = first_unit(w, p, 0)
                        if p == NT - 1:
                            last.then_inc(wk_used[w][0], 1)
                    a_gate_up(p, 0)
                for p in range(NT):
                    x_loaded(p, 1)
                    a_gate_up(p, 1).then_inc(a_products, 1)
                    last = first_unit(0, p, 1)
                last.then_inc(wk_used[0][1], 1)
                for p in range(NT):
                    last = first_unit(1, p, 1)
                last.then_inc(wk_used[1][1], 1)
                for w in range(2):
                    item_full(eng, h, BEFORE, (11, 13)[w])
                    adapters(ps[w], w, 0, (GATE_T, UP_T)[w])
                with eng.Fori(0, TURNS) as s:
                    turn(s, s)
                turn(AFTER, TURNS)

                b = BLOCKS - 1
                base = h * DOWNS + b * ADDS
                eng.wait_ge(down_added, START + base - 1)
                over_width(ps[2], 0, [(AFTER, 6), (AFTER, 7)])
                adapters(ps[2], 0, 1, GATE_T, stop=False)
                adapters(ps[2], 1, 1, UP_T)

                eng.wait_ge(act_full[0], START + h * BLOCKS + BLOCKS)
                eng.wait_ge(ad_full, START + h * BLOCKS + BLOCKS)
                item_full(eng, h, AFTER, 8)
                item_full(eng, h, AFTER, 9)
                eng.wait_ge(down_added, START + base)
                a_down(ps[3], 0, False, False)
                eng.wait_ge(silu_done[0], START + h * BLOCKS + BLOCKS)
                down_tile(ps[0], 0, 0)
                eng.wait_ge(mult_done[0], START + h * BLOCKS + BLOCKS)
                down_tile(ps[1], 1, 0)
                eng.wait_ge(mult_done[1], START + h * BLOCKS + BLOCKS)
                down_tile(ps[2], 2, 0)
                eng.wait_ge(act_full[1], START + h * BLOCKS + BLOCKS)
                a_down(ps[3], 1, True, True).then_inc(down_done, 1)
                for k in range(3):
                    down_tile_half(ps[down_pair(b, k + 1)], k)
                for k in range(3, KT):
                    dst = ps[down_pair(b, k + 1)]
                    eng.wait_ge(down_added, START + base + (k - 2))
                    down_tile(dst, k, 0)
                    down_tile_half(dst, k)
                    if k == 3:
                        item_full(eng, h, AFTER, 10)
                        item_full(eng, h, AFTER, 11)
                    for p in range(NT):
                        eng.wait_ge(t_full, h * T_PARTS + DOWN_T[p])
                        for t in (range(4) if k == 3 else [k]):
                            last = adapter(ps[down_pair(b, t + 1)], Wk[0][0:3 * Q, p, t, :], Tm[1], p)
                            if p == NT - 1:
                                last.then_inc(down_done, 1)

                eng.wait_ge(down_added, START + base + 6)
                item_full(eng, h, AFTER, AL)
                for k in range(KT):
                    eng.wait_ge(x1_full[k % 2], h * (KT // 2) + (k // 2 + 1))
                    for p in range(NT):
                        for l in range(2):
                            last = matmul(ps[0][0:2 * Q, tok(p)], Wk[1][:, 0, k, p * 2 * Q:(p + 1) * 2 * Q],
                                          X[:, l, k, tok(p)], start=(k == 0 and l == 0),
                                          stop=(k == KT - 1 and l == 1))
                        if k == KT - 1 and p == 0:
                            last.then_inc(a_products, 1)
                    if k % 4 == 3:
                        last.then_inc(wk_used[1][k // 4], 1)
                for k in range(KT):
                    dst = ps[out_pair(k)]
                    if k < 3:
                        eng.wait_ge(down_added, START + base + (7 + k))
                    elif k == 3:
                        eng.wait_ge(t_summed, h * T_PARTS + OUT_T[-1])
                    else:
                        eng.wait_ge(out_added, START + h * KT * NT + (k - 3) * NT)
                    for p in range(NT):
                        for g in range(2):
                            item_full(eng, h, AFTER, 14 + k + (2 if k >= 2 else 0), granules=g + 1)
                            last = tiles(dst, k % 2, range(4 * g, 4 * g + 4), pairs=[p])
                            if p == NT - 1:
                                last.then_inc(wk_used[k % 2][g], 1)
                        if k == 2 and p == 0:
                            for q in range(NT):
                                eng.wait_ge(t_full, h * T_PARTS + OUT_T[q])
                                item_full(eng, h, AFTER, 16 + q)
                            for t in range(2):
                                for q in range(NT):
                                    adapter(ps[out_pair(t)], Wd[0:3 * Q, 0, q, t, :], Tm[0], q
                                            ).then_inc(out_done, 1)
                        if k >= 2:
                            adapter(dst, Wd[0:3 * Q, 0, p, k, :], Tm[0], p).then_inc(out_done, 1)


_INS = ["x", "itok_B_2_6", "itok_B_1_7", "L0_cond_W_gate", "L0_cond_W_up", "L0_cond_W_down",
        "L0_cond_A_gate", "L0_cond_B_gate", "L0_cond_A_up", "L0_cond_B_up", "L0_cond_A_down", "L0_cond_B_down",
        "L1_cond_weight", "L1_cond_bias", "L1_cond_lora_a_weights", "L1_cond_lora_b_weights",
        "L1_cond_scaling_factors"]
_OUTS = [((8, 256, 1024), "float32")]


def kernel(**inputs):
    import numpy as _np
    import concourse.bacc as _bacc
    from concourse import mybir as _mybir
    from concourse.bass_utils import run_bass_kernel_spmd as _run

    nc = _bacc.Bacc("TRN2", target_bir_lowering=False, num_devices=1)
    arrays, args = {}, []
    for name in _INS:
        a = _np.ascontiguousarray(inputs[name])
        arrays[f"in_{name}_dram"] = a
        args.append(nc.dram_tensor(f"in_{name}_dram", a.shape, _mybir.dt.from_np(a.dtype), kind="ExternalInput").ap())
    for i, (shape, dtype) in enumerate(_OUTS):
        dt = _mybir.dt.from_np(_np.dtype(dtype))
        args.append(nc.dram_tensor(f"out_{i}_dram", shape, dt, kind="ExternalOutput").ap())
    build(nc, *args)
    r = _run(nc, [arrays], core_ids=[0])
    return r.results[0]["out_0_dram"]
```

```python
from contextlib import ExitStack

import concourse.bass as bass
from concourse import mybir

F32 = mybir.dt.float32
F32R = mybir.dt.float32r
ACT = mybir.ActivationFunctionType
ALU = mybir.AluOpType

P = 128
Q = 32
NQ = P // Q
RAW = 4
TURNED = 4
START = 2
BEFORE, AFTER = "before", "after"


class Tally:

    def __init__(self, before, body, after, turns):
        self.before, self.body, self.turns = before, body, turns
        self.total = before + turns * body + after

    def at(self, h, s, n):
        if s is BEFORE:
            return h * self.total + n
        if s is AFTER:
            return h * self.total + (self.before + self.turns * self.body + n)
        return h * self.total + s * self.body + (self.before + n)


def build(nc, x, l0_index, l1_index, w_gate, w_up, w_down, a_gate, b_gate, a_up, b_up, a_down, b_down,
          w_out, bias_in, a_out, b_out, scale_in, out):
    NB, NS, H = x.shape
    F = w_gate.shape[0]
    R = a_gate.shape[2]
    HALVES = 2
    BH = NB // HALVES
    T = BH * NS
    TT = 512
    NT = T // TT
    KT = H // P
    HQ = H // NQ
    FB = 256
    TURNS = F // FB - 1
    HC = P // 2
    ADDS = KT + 1
    assert (NS, TT, 2 * R, F % FB, F // FB) == (256, 2 * NS, Q, P + HC, 10)
    assert l0_index.shape[0] == NB and NT == 2 and KT == 8

    tokens = x.rearrange("b s h -> (b s) h")
    out_tokens = out.rearrange("b s h -> (b s) h")

    with ExitStack() as ctx:
        def sbuf(name, shape, dtype=F32):
            return ctx.enter_context(nc.sbuf_tensor(name, shape, dtype))

        def sem(name):
            return ctx.enter_context(nc.semaphore(name))

        X = sbuf("X", [P, 2, KT, T], F32R)
        acc = sbuf("acc", [P, ADDS, T])
        act = sbuf("act", [P, 2, 2, T], F32R)
        Wd = sbuf("Wd", [P, 2, 2, KT, P], F32R)
        Wk = [sbuf(f"Wk{j}", [P, 2, KT, P], F32R) for j in range(2)]
        raw = [sbuf(f"raw{j}", [P, 1024]) for j in range(RAW)]
        turned = [sbuf(f"turned{j}", [P, 1024]) for j in range(TURNED)]
        work = [sbuf(f"work{j}", [P, T]) for j in range(2)]
        Bf = sbuf("Bf", [96, 2, 2, 2, P], F32R)
        Ad_raw = sbuf("Ad_raw", [2 * Q, FB])
        Ad_turned = sbuf("Ad_turned", [P, 2, 2, Q])
        Ad = sbuf("Ad", [P, 2, 2, 2, Q], F32R)
        Tm = [sbuf(f"Tm{j}", [96, T], F32R) for j in range(2)]
        stage = [part.rearrange("p (t m) -> p t m", m=2 * Q) for part in (work[1][:, :], acc[:, KT, :])]
        indices = sbuf("indices", [1, 2 * NB], mybir.dt.int32)
        zeros = sbuf("zeros", [96, 2, HC])
        bias = sbuf("bias", [P, KT])
        scale_row = sbuf("scale_row", [Q, BH])
        pick = sbuf("pick", [Q, BH])
        pick_half = sbuf("pick_half", [Q, BH])
        pick_scale = sbuf("pick_scale", [Q, BH])

        ps = [ctx.enter_context(nc.psum_tensor(f"ps{j}", [P, T], F32)) for j in range(4)]

        raw_full = [sem(f"raw_full{j}") for j in range(RAW)]
        turned_full = [sem(f"turned_full{j}") for j in range(TURNED)]
        hi_full = [sem(f"hi_full{j}") for j in range(TURNED)]
        lo_full = [sem(f"lo_full{j}") for j in range(TURNED)]
        wk_used = [[sem(f"wk_used{j}{g}") for g in range(2)] for j in range(2)]
        ad_loaded, ad_turned, ad_hi, ad_full = (sem(n) for n in ("ad_loaded", "ad_turned", "ad_hi", "ad_full"))
        unit_done = [[sem(f"unit_done{w}{c}") for c in range(2)] for w in range(2)]
        silu_done = [sem(f"silu_done{c}") for c in range(2)]
        mult_done = [sem(f"mult_done{c}") for c in range(2)]
        act_hi = [sem(f"act_hi{c}") for c in range(2)]
        act_full = [sem(f"act_full{c}") for c in range(2)]
        t_copied, t_summed, t_masked, t_hi, t_again, t_full = (sem(n) for n in (
            "t_copied", "t_summed", "t_masked", "t_hi", "t_again", "t_full"))
        down_done, down_added = sem("down_done"), sem("down_added")
        a_products = sem("a_products")
        down_t = sem("down_t")
        acc_set = sem("acc_set")
        x1_hi = sem("x1_hi")
        x1_full = [sem(f"x1_full{j}") for j in range(2)]
        out_done, out_added, out_turned = (sem(n) for n in ("out_done", "out_added", "out_turned"))
        out_stored = [sem(f"out_stored{m}") for m in range(2)]
        indices_loaded = sem("indices_loaded")
        bias_loaded, pick_set, pick_ready, zeros_set = (sem(n) for n in (
            "bias_loaded", "pick_set", "pick_ready", "zeros_set"))

        BLOCKS = TURNS + 2
        ITEMS_BEFORE, TURN_ITEMS, ITEMS_AFTER = 16, 8, 24
        FIRST_ITEMS = ["G", "x0", "x1", "U", "Agu0", "x2", "x3", "Agu1", "x4", "x5", "x6", "Bg", "x7", "Bu"]
        X_AT = [FIRST_ITEMS.index(f"x{i}") for i in range(8)]
        X_BY_VECTOR = {X_AT[1]: (X_AT[0], X_AT[1]), X_AT[5]: (X_AT[4],), X_AT[6] + 1: (X_AT[6],)}
        AGU = [FIRST_ITEMS.index(f"Agu{p}") for p in range(NT)]
        AL = 12
        X1_BY_VECTOR = [1, 3, 5, 6, 7]
        DMAS = 4
        CHUNKS = [2 * BLOCKS, 2 * BLOCKS - 1]
        WK_USED = [CHUNKS[0] + KT // 2, CHUNKS[1] + 1 + KT // 2]
        DOWNS = BLOCKS * ADDS
        A_PRODUCTS = NT + 1
        T_PARTS = 4 * NT
        GATE_T, UP_T, DOWN_T, OUT_T = (1, 3), (2, 4), (5, 6), (7, 8)

        def in_ring(ring, h, s, n):
            return n % ring, Tally(ITEMS_BEFORE // ring, TURN_ITEMS // ring, ITEMS_AFTER // ring, TURNS).at(
                h, s, n // ring)

        def turned_at(h, s, n):
            return in_ring(TURNED, h, s, n)

        def chunk_at(h, c, blocks):
            return START + h * (BLOCKS + c * (NT - 1)) + blocks

        def half_chunk_at(h, p):
            return chunk_at(h, 1, BLOCKS - 1) + p + 1

        def item_full(eng, h, s, n, granules=2):
            j, before = turned_at(h, s, n)
            eng.wait_ge(lo_full[j], START + before * 2 + granules)

        def down_pair(b, i):
            if isinstance(b, int) and b == BLOCKS - 1:
                return (3 + i) % 4
            return 3 - i % 2

        def out_pair(k):
            return (k + 1) % 4

        block = ctx.enter_context(nc.Block())

        @block.sync
        def _(sp):
            with sp.Fori(0, HALVES) as h:
                def batch_indices(table, rows):
                    return [sp.value_load(indices[:, bass.ds(h * BH + (table * NB + b), 1)], min_val=0,
                                          max_val=rows - 1) for b in range(BH)]

                def slot(s, n):
                    last = n - RAW
                    if s is BEFORE and last < 0:
                        for j in range(TURNED):
                            sp.wait_ge(turned_full[j], START + turned_at(h, BEFORE, 0)[1])
                    else:
                        j, before = turned_at(h, s, last)
                        sp.wait_ge(turned_full[j], START + before + 1)
                    return raw[n % RAW], raw_full[n % RAW]

                def load_rows(s, n, w, group, step, nq):
                    buf, full = slot(s, n)
                    rows = w.rearrange("(g i) m -> i g m", i=Q)
                    for c in range(NQ):
                        sp.dma_start(buf[c * Q:(c + 1) * Q, 0:nq * HQ].rearrange("i (q m) -> i q m", q=nq),
                                     rows[:, bass.ds(group, nq, step), c * HQ:(c + 1) * HQ]).then_inc(full, 16)

                def load_down(s, n, e, b):
                    buf, full = slot(s, n)
                    rows = w_down.rearrange("(g i) f -> i g f", i=Q)
                    for q in range(NQ):
                        sp.dma_start(buf[q * Q:(q + 1) * Q, :].rearrange("i (g f) -> i g f", f=2 * Q),
                                     rows[:, 16 * e:16 * e + 16, bass.ds(b * FB + q * 2 * Q, 2 * Q)]
                                     ).then_inc(full, 16)

                def load_last_down(n, c):
                    buf, full = slot(AFTER, n)
                    rows = w_down.rearrange("(g i) f -> i g f", i=Q)
                    for q in range(NQ):
                        first = (BLOCKS - 1) * FB + c * P + (q % 2 if c else q) * Q
                        sp.dma_start(buf[q * Q:(q + 1) * Q, :].rearrange("i (g f) -> i g f", f=Q),
                                     rows[:, :, first:first + Q]).then_inc(full, 16)

                def load_b(s, n, b_all, f0, each):
                    buf, full = slot(s, n)
                    for b in range(BH):
                        src = b_all[0, bass.ds(l0[b], 1), bass.ds(f0, Q * each), :]
                        sp.dma_start(buf[0:Q, b * 128:b * 128 + each * R],
                                     src.rearrange("o (i j) r -> (o i) (j r)", i=Q)).then_inc(full, 16)

                def load_b_pair(s, n, b_all, index, p):
                    buf, full = slot(s, n)
                    for b in range(2):
                        src = b_all[bass.ds(index[2 * p + b], 1), :, :].rearrange("o (i j) r -> (o i) (j r)", i=Q)
                        for m in range(2):
                            sp.dma_start(buf[0:Q, b * 512 + m * 256:b * 512 + (m + 1) * 256],
                                         src[:, m * 256:(m + 1) * 256]).then_inc(full, 16)

                def load_a(s, n, parts):
                    buf, full = slot(s, n)
                    for g, (a_all, index) in enumerate(parts):
                        sp.dma_start(buf[g * R:(g + 1) * R, :],
                                     a_all[bass.ds(index, 1), :, :].rearrange("o r m -> (o r) m")
                                     ).then_inc(full, 16)

                def load_ad(b, features):
                    for i in range(BH):
                        src = a_down[0, bass.ds(l0[i], 1), :, bass.ds(b * FB, features)]
                        sp.dma_start(Ad_raw[i * R:(i + 1) * R, 0:features],
                                     src.rearrange("o r m -> (o r) m")).then_inc(ad_loaded, 16)

                def load_turn(s, b, last=False):
                    load_down(s, 0, 0, b)
                    load_down(s, 1, 1, b)
                    sp.wait_ge(ad_turned, START + h * BLOCKS + b)
                    load_ad(b, FB)
                    first = (b + 1) * (FB // Q)
                    second, step, nq, each = (first + 4, 1, 2, 6) if last else (first + 1, 2, NQ, 8)
                    load_rows(s, 2, w_gate, first, step, NQ)
                    load_b(s, 3, b_gate, (b + 1) * FB, each)
                    load_rows(s, 4, w_up, first, step, NQ)
                    load_b(s, 5, b_up, (b + 1) * FB, each)
                    load_rows(s, 6, w_gate, second, step, nq)
                    load_rows(s, 7, w_up, second, step, nq)

                def load_x(n):
                    first_col, first_token = n // 4 * 128, n % 4 * 256
                    buf, full = slot(BEFORE, X_AT[n])
                    for c in range(NQ):
                        col = c * HQ + first_col
                        src = tokens[bass.ds(h * T + first_token, 256), col:col + 128]
                        sp.dma_start(buf[c * Q:(c + 1) * Q, :].rearrange("i (t m) -> i t m", t=8),
                                     src.rearrange("(t i) m -> i t m", i=Q)).then_inc(full, 16)

                def load_agu(p):
                    load_a(BEFORE, AGU[p], [(a, l0[2 * p + b]) for a in (a_gate[0], a_up[0]) for b in range(2)])

                load_rows(BEFORE, 0, w_gate, 0, 2, NQ)
                load_x(0)
                load_x(1)
                load_rows(BEFORE, 3, w_up, 0, 2, NQ)
                sp.wait_ge(indices_loaded, 2 * 16)
                l0 = batch_indices(0, a_gate.shape[1])
                load_agu(0)
                load_x(2)
                load_x(3)
                load_agu(1)
                load_x(4)
                load_x(5)
                load_x(6)
                load_b(BEFORE, 11, b_gate, 0, 8)
                load_x(7)
                load_b(BEFORE, 13, b_up, 0, 8)
                load_rows(BEFORE, 14, w_gate, 1, 2, NQ)
                load_rows(BEFORE, 15, w_up, 1, 2, NQ)
                with sp.Fori(0, TURNS) as s:
                    load_turn(s, s)
                load_turn(AFTER, TURNS, last=True)
                l1 = batch_indices(1, a_out.shape[0])
                load_last_down(8, 0)
                load_last_down(9, 1)
                sp.wait_ge(ad_turned, START + h * BLOCKS + (BLOCKS - 1))
                load_ad(BLOCKS - 1, P + HC)
                load_b_pair(AFTER, 10, b_down[0], l0, 0)
                load_b_pair(AFTER, 11, b_down[0], l0, 1)
                buf, full = slot(AFTER, 13)
                load_a(AFTER, AL, [(a_out, l1[b]) for b in range(BH)])
                for b in range(BH):
                    factor = scale_in.rearrange("(n o) -> n o", o=1)[bass.ds(l1[b], 1), :]
                    sp.dma_start(buf[0:Q, b:b + 1], factor.to_broadcast([Q, 1]),
                                 allow_slow_non_contiguous=True).then_inc(full, 16)
                for k in range(KT):
                    if k == 2:
                        load_b_pair(AFTER, 16, b_out, l1, 0)
                        load_b_pair(AFTER, 17, b_out, l1, 1)
                    load_rows(AFTER, 14 + k + (2 if k >= 2 else 0), w_out, k, KT, NQ)

        def places(item, g, j, last=False, k_out=0):
            src, ks = turned[j], slice(4 * g, 4 * g + 4)
            if item in ("G", "U", "O"):
                wk = Wk[{"G": 0, "U": 1, "O": k_out % 2}[item]]
                return (src[:, :].rearrange("p (k m) -> p k m", k=KT)[:, ks, :],
                        [wk[:, 0, ks, :]], wk[:, 1, ks, :])
            if item in ("Gh", "Uh"):
                cols = slice(0, HC) if item == "Gh" else slice(HC, P)
                return (src[:, 0:KT * HC].rearrange("p (k m) -> p k m", k=KT)[:, ks, :],
                        [Wk[0][:, 0, ks, cols]], Wk[0][:, 1, ks, cols])
            if item in ("Agu0", "Agu1", "Al"):
                home = (Wk[1][:, 0] if item == "Al" else Wd[:, 1, int(item[3])])[:, ks, :]
                home = home.rearrange("p k (w l r) -> p k w l r", w=2, l=2)
                return (src[:, 0:512].rearrange("p (k w r) -> p k w r", k=KT, w=2)[:, ks, :, :],
                        [home[:, :, :, 0, :]], home[:, :, :, 1, :])
            if item[0] == "D":
                c, e = (int(item[2]), g) if item[1] == "c" else (g, int(item[1]))
                hi_lo = [Wd[:, c, l, :, e * 64:(e + 1) * 64].rearrange("p k (q i) -> p q k i", q=2)
                         for l in range(2)]
                return (src[:, g * 512:(g + 1) * 512].rearrange("p (q k i) -> p q k i", q=2, k=KT),
                        [hi_lo[0]], hi_lo[1])
            if item in ("Bg", "Bu"):
                w = "gu".index(item[1])
                cols = slice(w * HC, (w + 1) * HC) if last and g else slice(0, P)
                rows = [Bf[r * Q:(r + 1) * Q, w, g, :, cols].rearrange("p w (q i) -> p w q i", i=Q)
                        for r in range(3)]
                src = src[0:Q, 0:2 * FB]
                if last:
                    src = src.rearrange("p (w q i) -> p w q i", w=2, i=Q)[:, :, 4 * g:4 * g + (2 if g else 4), :]
                else:
                    src = src.rearrange("p (w q c i) -> p w q c i", w=2, q=NQ, c=2)[:, :, :, g, :]
                return src, rows[0:2], rows[2]
            if item[0] == "x":
                n = int(item[1])
                ks, ts = slice(n // 4 * 4 + 2 * g, n // 4 * 4 + 2 * g + 2), slice(n % 4 * 256, n % 4 * 256 + 256)
                return (src[:, :].rearrange("p (k t) -> p k t", k=4)[:, 2 * g:2 * g + 2, :],
                        [X[:, 0, ks, ts]], X[:, 1, ks, ts])
            if item == "scale":
                return src[0:Q, 2 * g:2 * g + 2], [scale_row[:, 2 * g:2 * g + 2]], pick_scale[:, 2 * g:2 * g + 2]
            p = int(item[2])
            home = Wk[0][:, p] if item[1] == "d" else Wd[:, 0, p]
            rows = [home[r * Q:(r + 1) * Q, ks, :].rearrange("p k (q i) -> p q k i", q=NQ) for r in range(3)]
            return (src[0:Q, :].rearrange("p (q k i) -> p q k i", q=NQ, k=KT)[:, :, ks, :], rows[0:2], rows[2])

        def acc_start(engine, k):
            engine.tensor_tensor(acc[:, k, :], X[:, 0, k, :].bitcast(F32), X[:, 1, k, :].bitcast(F32), ALU.add
                                 ).then_inc(acc_set, 1)

        @block.scalar
        def _(eng):
            for n, table in enumerate((l0_index, l1_index)):
                eng.dma_start(indices[:, n * NB:(n + 1) * NB], table.rearrange("(o n) -> o n", o=1)
                              ).then_inc(indices_loaded, 16)
            for sem_ in (*silu_done, *act_hi, *out_stored):
                eng.sem_inc(sem_, START)
            eng.wait_ge(zeros_set, 1)
            with eng.Fori(0, HALVES) as h:
                def home_free(item, g, n):
                    if item in ("Agu0", "Agu1"):
                        eng.wait_ge(down_done, START + h * DOWNS)
                    elif item[0] == "x":
                        eng.wait_ge(wk_used[1][int(item[1]) // 4], START + h * WK_USED[1])
                    elif item in ("G", "Gh", "Uh"):
                        eng.wait_ge(wk_used[0][g], START + h * WK_USED[0] + n)
                    elif item == "U":
                        eng.wait_ge(wk_used[1][g], START + h * WK_USED[1] + n)
                    elif item in ("Bg", "Bu"):
                        eng.wait_ge(unit_done["gu".index(item[1])][g], chunk_at(h, g, n))
                    elif item[0] == "D":
                        eng.wait_ge(down_done, START + h * DOWNS + n * ADDS)
                        eng.wait_ge(a_products, h * A_PRODUCTS + NT)
                        eng.wait_ge(out_done, START + h * KT * NT)
                    elif item in ("Bd0", "Bd1"):
                        for gg in range(2):
                            eng.wait_ge(wk_used[0][gg], START + h * WK_USED[0] + CHUNKS[0])
                    elif item == "Al":
                        eng.wait_ge(wk_used[1][g], START + h * WK_USED[1] + CHUNKS[1])
                    elif item == "O":
                        eng.wait_ge(wk_used[n % 2][g], START + h * WK_USED[n % 2] + (CHUNKS[n % 2] + n % 2 + n // 2))
                        eng.wait_ge(down_done, START + h * DOWNS + DOWNS)
                    elif item in ("Bl0", "Bl1"):
                        eng.wait_ge(down_done, START + h * DOWNS + DOWNS)

                def hi(s, n, item, at=0, last_b=False):
                    j, before = turned_at(h, s, n)
                    eng.wait_ge(turned_full[j], START + before + 1)
                    for g in range(2):
                        home_free(item, g, at)
                        src, homes, _ = places(item, g, j, last_b, at)
                        if last_b and g:
                            w = "gu".index(item[1])
                            nc.scalar.activation(Bf[:, w, g, :, (1 - w) * HC:(2 - w) * HC], zeros[:, :, :], ACT.Copy)
                        for home in homes:
                            last = nc.scalar.activation(home, src, ACT.Copy)
                        last.then_inc(hi_full[j], 1)

                def silu(c, b):
                    eng.wait_ge(unit_done[0][c], chunk_at(h, c, b + 1))
                    eng.wait_ge(act_full[c], chunk_at(h, c, b))
                    eng.wait_ge(t_full, h * T_PARTS + 2 * NT)
                    nc.scalar.activation(work[c][:, :], ps[2 * c][:, :], ACT.Silu).then_inc(silu_done[c], 1)

                def act_high(c, b):
                    eng.wait_ge(mult_done[c], chunk_at(h, c, b + 1))
                    eng.wait_ge(down_done, START + h * DOWNS + b * ADDS)
                    nc.scalar.activation(act[:, c, 0, :], work[c][:, :], ACT.Copy).then_inc(act_hi[c], 1)

                def silu_half(p):
                    ts = slice(p * TT, (p + 1) * TT)
                    eng.wait_ge(unit_done[1][1], half_chunk_at(h, p))
                    nc.scalar.activation(work[1][0:HC, ts], ps[2][0:HC, ts], ACT.Silu).then_inc(silu_done[1], 1)

                def act_high_half(p):
                    ts = slice(p * TT, (p + 1) * TT)
                    eng.wait_ge(mult_done[1], half_chunk_at(h, p))
                    eng.wait_ge(down_done, START + h * DOWNS + (BLOCKS - 1) * ADDS)
                    nc.scalar.activation(act[0:HC, 1, 0, ts], work[1][0:HC, ts], ACT.Copy).then_inc(act_hi[1], 1)

                def ad_high(b):
                    eng.wait_ge(ad_turned, START + h * BLOCKS + b + 1)
                    eng.wait_ge(down_done, START + h * DOWNS + b * ADDS)
                    nc.scalar.activation(Ad[:, :, :, 0, :], Ad_turned[:, :, :, :], ACT.Copy).then_inc(ad_hi, 1)

                def t_copy(src, w, p):
                    ts = slice(p * TT, (p + 1) * TT)
                    nc.scalar.activation(work[w][0:Q, ts], src[:, ts], ACT.Copy).then_inc(t_copied, 1)

                def t_high(w, p, part):
                    ts = slice(p * TT, (p + 1) * TT)
                    eng.wait_ge(t_masked, h * T_PARTS + part)
                    nc.scalar.activation(Tm[w][0:Q, ts], work[w][0:Q, ts], ACT.Copy).then_inc(t_hi, 1)
                    nc.scalar.activation(Tm[w][2 * Q:3 * Q, ts], work[w][0:Q, ts], ACT.Copy).then_inc(t_again, 1)

                def turn(s, b, last=False):
                    act_high(0, b)
                    hi(s, 0, "D0", b)
                    hi(s, 1, "D1", b)
                    ad_high(b)
                    hi(s, 2, "G", 2 * b + 2)
                    silu(1, b)
                    hi(s, 3, "Bg", b + 1, last)
                    hi(s, 4, "U", 2 * b + 2)
                    act_high(1, b)
                    hi(s, 5, "Bu", b + 1, last)
                    silu(0, b + 1)
                    hi(s, 6, "Gh" if last else "G", 2 * b + 3)
                    hi(s, 7, "Uh" if last else "U", 2 * b + 3)

                for n, item in enumerate(FIRST_ITEMS):
                    hi(BEFORE, n, item)
                eng.wait_ge(out_stored[0], START + h * (KT // 2 * NQ * 16))
                for p in range(NT):
                    eng.wait_ge(a_products, h * A_PRODUCTS + (p + 1))
                    t_copy(ps[2][Q:2 * Q, :], 0, p)
                    t_copy(ps[2][3 * Q:4 * Q, :], 1, p)
                for p in range(NT):
                    t_high(0, p, GATE_T[p])
                    t_high(1, p, UP_T[p])
                    if p == 0:
                        hi(BEFORE, 14, "G", 1)
                hi(BEFORE, 15, "U", 1)
                silu(0, 0)
                with eng.Fori(0, TURNS) as s:
                    turn(s, s)
                turn(AFTER, TURNS, last=True)

                act_high(0, BLOCKS - 1)
                hi(AFTER, 8, "Dc0", BLOCKS - 1)
                hi(AFTER, 9, "Dc1", BLOCKS - 1)
                ad_high(BLOCKS - 1)
                eng.wait_ge(act_full[1], chunk_at(h, 1, BLOCKS - 1))
                silu_half(0)
                act_high_half(0)
                hi(AFTER, 10, "Bd0")
                silu_half(1)
                act_high_half(1)
                hi(AFTER, 11, "Bd1")
                eng.wait_ge(act_full[1], chunk_at(h, 1, BLOCKS + NT - 1))
                eng.wait_ge(down_t, h + 1)
                t_copy(acc[Q:2 * Q, KT, :], 1, 0)
                eng.wait_ge(down_added, START + h * DOWNS + ((BLOCKS - 1) * ADDS + 1))
                t_copy(acc[Q:2 * Q, KT, :], 1, 1)
                for p in range(NT):
                    t_high(1, p, DOWN_T[p])
                for k in range(KT):
                    if k == 4:
                        hi(AFTER, AL, "Al")
                    elif k == 5:
                        hi(AFTER, 13, "scale")
                    eng.wait_ge(down_added, START + h * DOWNS + (BLOCKS - 1) * ADDS + 2 + k)
                    nc.scalar.activation(X[:, 0, k, :], acc[:, k, :], ACT.Copy).then_inc(x1_hi, 1)
                hi(AFTER, 14, "O", 0)
                eng.wait_ge(a_products, h * A_PRODUCTS + NT + 1)
                t_copy(ps[0][Q:2 * Q, :], 0, 0)
                eng.wait_ge(wk_used[1][1], START + h * WK_USED[1] + (CHUNKS[1] + 1))
                t_copy(ps[0][Q:2 * Q, :], 0, 1)
                hi(AFTER, 15, "O", 1)
                hi(AFTER, 16, "Bl0")
                for p in range(NT):
                    t_high(0, p, OUT_T[p])
                hi(AFTER, 17, "Bl1")

                def store(pair):
                    for m in range(2):
                        eng.wait_ge(out_turned, START + h * KT + (2 * pair + m + 1))
                        for q in range(NQ):
                            col = q * HQ + pair * 2 * Q
                            rows = out_tokens[bass.ds(h * T + m * TT, TT), col:col + 2 * Q]
                            eng.dma_start(rows.rearrange("(t i) m -> i t m", i=Q),
                                          stage[m][q * Q:(q + 1) * Q, :, :]).then_inc(out_stored[m], 16)

                for k in range(KT):
                    if k + 2 < KT:
                        hi(AFTER, 18 + k, "O", k + 2)
                    if k % 2:
                        store(k // 2)
            for m in range(2):
                eng.wait_ge(out_stored[m], START + HALVES * (KT // 2) * NQ * 16)

        @block.gpsimd
        def _(eng):
            for sem_ in (*lo_full, ad_full):
                eng.sem_inc(sem_, START)
            for q in range(NQ):
                eng.dma_start(bias[q * Q:(q + 1) * Q, :],
                              bias_in.rearrange("(q k i) -> q i k", q=NQ, k=KT)[q],
                              allow_slow_non_contiguous=True).then_inc(bias_loaded, 16)
            eng.memset(zeros[:, :, :], 0.0).then_inc(zeros_set, 1)
            eng.memset(pick[:, :], 1.0).then_inc(pick_set, 1)
            eng.wait_ge(pick_set, 1)
            parity = pick[:, :].rearrange("p (w b) -> p w b", b=2)
            eng.affine_select(out=parity[:, :, 0], in_=parity[:, :, 0], compare_op=ALU.is_ge, fill=0.0,
                              base=R - 1, pattern=[[0, 2]], channel_multiplier=-1).then_inc(pick_set, 1)
            eng.affine_select(out=parity[:, :, 1], in_=parity[:, :, 1], compare_op=ALU.is_ge, fill=0.0,
                              base=-R, pattern=[[0, 2]], channel_multiplier=1).then_inc(pick_set, 1)
            eng.wait_ge(pick_set, 3)
            nc.gpsimd.tensor_scalar(pick_half[:, :], pick[:, :], 0.5, None, ALU.mult).then_inc(pick_ready, 1)
            with eng.Fori(0, HALVES) as h:
                def lo(s, n, item, at=0, last_b=False):
                    j, before = turned_at(h, s, n)
                    across = item[0] == "B"
                    if across:
                        for earlier in (n - 2, n - 1):
                            item_full(eng, h, s, earlier)
                        if item == "Bd0":
                            eng.wait_ge(ad_full, START + h * BLOCKS + BLOCKS)
                    for g in range(2):
                        eng.wait_ge(hi_full[j], before * 2 + (g + 1))
                        src, homes, home = places(item, g, j, last_b, at)
                        if item == "scale":
                            nc.gpsimd.tensor_tensor(home, homes[0], pick[:, 2 * g:2 * g + 2],
                                                    ALU.mult).then_inc(lo_full[j], 1)
                        else:
                            nc.gpsimd.tensor_tensor(home, src, homes[0].bitcast(F32),
                                                    ALU.subtract).then_inc(lo_full[j], 1)
                        if across:
                            item_full(eng, h, s, n, granules=g + 1)

                def ad_low(b):
                    eng.wait_ge(ad_hi, h * BLOCKS + b + 1)
                    nc.gpsimd.tensor_tensor(Ad[:, :, :, 1, :], Ad_turned[:, :, :, :],
                                            Ad[:, :, :, 0, :].bitcast(F32), ALU.subtract).then_inc(ad_full, 1)

                def x1_low(k):
                    eng.wait_ge(x1_hi, h * KT + k + 1)
                    nc.gpsimd.tensor_tensor(X[:, 1, k, :], acc[:, k, :], X[:, 0, k, :].bitcast(F32),
                                            ALU.subtract).then_inc(x1_full[0], 1)

                def turn(s, b, last=False):
                    lo(s, 0, "D0")
                    lo(s, 1, "D1")
                    ad_low(b)
                    for n, item in enumerate(("G", "Bg", "U", "Bu", "Gh" if last else "G", "Uh" if last else "U")):
                        lo(s, 2 + n, item, last_b=last)

                for n, item in enumerate(FIRST_ITEMS):
                    if all(n not in of_x for of_x in X_BY_VECTOR.values()):
                        lo(BEFORE, n, item)
                lo(BEFORE, 14, "G")
                lo(BEFORE, 15, "U")
                eng.wait_ge(out_turned, START + h * KT)
                for n in X_AT:
                    item_full(eng, h, BEFORE, n)
                for k in range(KT // 2):
                    acc_start(nc.gpsimd, k)
                with eng.Fori(0, TURNS) as s:
                    turn(s, s)
                turn(AFTER, TURNS, last=True)
                lo(AFTER, 8, "Dc0")
                lo(AFTER, 9, "Dc1")
                ad_low(BLOCKS - 1)
                lo(AFTER, 10, "Bd0")
                lo(AFTER, 11, "Bd1")
                x1_low(0)
                x1_low(2)
                lo(AFTER, AL, "Al")
                x1_low(4)
                lo(AFTER, 13, "scale")
                lo(AFTER, 14, "O", 0)
                lo(AFTER, 15, "O", 1)
                lo(AFTER, 16, "Bl0")
                lo(AFTER, 17, "Bl1")
                for k in range(2, KT):
                    lo(AFTER, 16 + k, "O", k)

        @block.vector
        def _(eng):
            for sem_ in (*turned_full, ad_turned, *act_full, *mult_done, down_added, out_turned, out_added):
                eng.sem_inc(sem_, START)
            with eng.Fori(0, HALVES) as h:
                def turn_item(s, n, item, nq=NQ):
                    j, before = turned_at(h, s, n)
                    jr, loaded = in_ring(RAW, h, s, n)
                    eng.wait_ge(raw_full[jr], (loaded + 1) * (DMAS * 16))
                    eng.wait_ge(lo_full[j], START + before * 2)
                    src, dst = raw[jr], turned[j]
                    if item in ("G", "U", "Gh", "Uh", "O"):
                        last = nc.vector.transpose(
                            dst[:, 0:KT * nq * Q].rearrange("p (k q i) -> p k q i", k=KT, q=nq),
                            src[:, 0:nq * HQ].rearrange("p (q k i) -> p k q i", q=nq, k=KT))
                    elif item in ("Agu0", "Agu1", "Al"):
                        for w in range(2):
                            for q in range(NQ):
                                last = nc.vector.transpose(
                                    dst[q * Q:(q + 1) * Q, 0:512].rearrange(
                                        "p (k w i) -> p k w i", k=KT, w=2)[:, :, w, :],
                                    src[w * Q:(w + 1) * Q, q * HQ:(q + 1) * HQ].rearrange(
                                        "p (k i) -> p k i", k=KT))
                    elif item[0] == "x":
                        last = nc.vector.transpose(dst[:, :].rearrange("p (k t i) -> p k t i", k=4, t=8),
                                                   src[:, :].rearrange("p (t k i) -> p k t i", t=8, k=4))
                    elif item in ("Dc0", "Dc1"):
                        last = nc.vector.transpose(dst[:, :], src[:, :])
                    elif item in ("D0", "D1"):
                        last = nc.vector.transpose(
                            dst[:, :].rearrange("p (c g i) -> p c g i", c=2, g=16),
                            src[:, :].rearrange("p (g c i) -> p c g i", g=16, c=2))
                    elif item in ("Bg", "Bu"):
                        each = 2 * nq
                        for w in range(NT):
                            last = nc.vector.transpose(
                                dst[0:Q, w * FB:w * FB + Q * each].rearrange("p (i j) -> p j i", j=each),
                                src[0:Q, w * FB:(w + 1) * FB].rearrange("p (b j r) -> p j b r", b=2, r=R)[
                                    :, 0:each, :, :])
                    elif item == "scale":
                        last = nc.vector.tensor_copy(dst[0:Q, 0:BH], src[0:Q, 0:BH])
                    else:
                        last = nc.vector.transpose(
                            dst[0:Q, :].rearrange("p (i j) -> p j i", j=Q),
                            src[0:Q, :].rearrange("p (b j r) -> p j b r", b=2, r=R))
                    last.then_inc(turned_full[j], 1)

                def item_low(n, item):
                    j, before = turned_at(h, BEFORE, n)
                    for g in range(2):
                        eng.wait_ge(hi_full[j], before * 2 + (g + 1))
                        src, homes, home = places(item, g, j)
                        nc.vector.tensor_tensor(home, src, homes[0].bitcast(F32), ALU.subtract
                                                ).then_inc(lo_full[j], 1)

                def turn_ad(b, last=False):
                    eng.wait_ge(ad_loaded, (h * BLOCKS + b + 1) * BH * 16)
                    eng.wait_ge(ad_full, START + h * BLOCKS + b)
                    for w in range(NT):
                        for q in range(NQ):
                            groups = slice(q, q + 5 - q // 2 * 2, 4 - q // 2 * 2) if last else slice(2 * q, 2 * q + 2)
                            done = nc.vector.transpose(
                                Ad_turned[q * Q:(q + 1) * Q, :, w, :],
                                Ad_raw[w * Q:(w + 1) * Q, :].rearrange("p (z i) -> p z i", i=Q)[:, groups, :])
                    done.then_inc(ad_turned, 1)

                def multiply(c, b):
                    eng.wait_ge(unit_done[1][c], chunk_at(h, c, b + 1))
                    eng.wait_ge(silu_done[c], chunk_at(h, c, b + 1))
                    nc.vector.tensor_tensor(work[c][:, :], work[c][:, :], ps[2 * c + 1][:, :], ALU.mult
                                            ).then_inc(mult_done[c], 1)

                def act_low(c, b):
                    eng.wait_ge(act_hi[c], chunk_at(h, c, b + 1))
                    nc.vector.tensor_tensor(act[:, c, 1, :], work[c][:, :], act[:, c, 0, :].bitcast(F32),
                                            ALU.subtract).then_inc(act_full[c], 1)

                def t_sum(src, w, p, part, factors):
                    one = work[w][0:Q, p * TT:(p + 1) * TT]
                    eng.wait_ge(t_copied, h * T_PARTS + part)
                    nc.vector.tensor_tensor(one, one, src[:, p * TT:(p + 1) * TT], ALU.add).then_inc(t_summed, 1)
                    eng.wait_ge(t_summed, h * T_PARTS + part)
                    one = one.rearrange("p (b t) -> p b t", b=2)
                    nc.vector.tensor_tensor(one, one, factors[:, 2 * p:2 * p + 2].unsqueeze(2).to_broadcast([Q, 2, NS]),
                                            ALU.mult).then_inc(t_masked, 1)

                def t_low(w, p, part):
                    ts = slice(p * TT, (p + 1) * TT)
                    eng.wait_ge(t_hi, h * T_PARTS + part)
                    nc.vector.tensor_tensor(Tm[w][Q:2 * Q, ts], work[w][0:Q, ts], Tm[w][0:Q, ts].bitcast(F32),
                                            ALU.subtract).then_inc(t_full, 1)

                def x1_low(k):
                    eng.wait_ge(x1_hi, h * KT + k + 1)
                    nc.vector.tensor_tensor(X[:, 1, k, :], acc[:, k, :], X[:, 0, k, :].bitcast(F32),
                                            ALU.subtract).then_inc(x1_full[1], 1)

                def add_down(b, i):
                    base = h * DOWNS + b * ADDS
                    pair = down_pair(b, i)
                    eng.wait_ge(down_done, START + base + i + 1)
                    dst = acc[0:2 * Q, KT, :] if i == 0 else acc[:, i - 1, :]
                    src = ps[pair][0:2 * Q, :] if i == 0 else ps[pair][:, :]
                    nc.vector.tensor_tensor(dst, dst, src, ALU.add).then_inc(down_added, 1)

                def turn(s, b, last=False):
                    act_low(0, b)
                    turn_item(s, 0, "D0")
                    turn_item(s, 1, "D1")
                    turn_ad(b)
                    turn_item(s, 2, "G")
                    turn_item(s, 3, "Bg", 3 if last else NQ)
                    turn_item(s, 4, "U")
                    multiply(1, b)
                    act_low(1, b)
                    turn_item(s, 5, "Bu", 3 if last else NQ)
                    turn_item(s, 6, "Gh" if last else "G", 2 if last else NQ)
                    turn_item(s, 7, "Uh" if last else "U", 2 if last else NQ)
                    multiply(0, b + 1)
                    eng.wait_ge(down_added, START + h * DOWNS + b * ADDS)
                    eng.wait_ge(acc_set, h * (KT + 1) + (KT + 1))
                    for i in range(ADDS):
                        add_down(b, i)

                for n, item in enumerate(FIRST_ITEMS):
                    turn_item(BEFORE, n, item)
                    for of_x in X_BY_VECTOR.get(n, ()):
                        item_low(of_x, FIRST_ITEMS[of_x])
                eng.wait_ge(pick_ready, 1)
                turn_item(BEFORE, 14, "G")
                for p in range(NT):
                    t_sum(ps[2][0:Q, :], 0, p, GATE_T[p], pick_half)
                    t_sum(ps[2][2 * Q:3 * Q, :], 1, p, UP_T[p], pick_half)
                for p in range(NT):
                    t_low(0, p, GATE_T[p])
                    t_low(1, p, UP_T[p])
                turn_item(BEFORE, 15, "U")
                eng.wait_ge(out_stored[1], START + h * (KT // 2 * NQ * 16))
                nc.vector.memset(acc[0:2 * Q, KT, :], 0.0).then_inc(acc_set, 1)
                for n in X_AT:
                    item_full(eng, h, BEFORE, n)
                for k in range(KT // 2, KT):
                    acc_start(nc.vector, k)
                multiply(0, 0)
                with eng.Fori(0, TURNS) as s:
                    turn(s, s)
                turn(AFTER, TURNS, last=True)

                b = BLOCKS - 1
                act_low(0, b)
                turn_item(AFTER, 8, "Dc0")
                turn_item(AFTER, 9, "Dc1")
                turn_ad(b, last=True)
                turn_item(AFTER, 10, "Bd0")
                turn_item(AFTER, 11, "Bd1")
                for p in range(NT):
                    ts = slice(p * TT, (p + 1) * TT)
                    eng.wait_ge(silu_done[1], half_chunk_at(h, p))
                    nc.vector.tensor_tensor(work[1][0:HC, ts], work[1][0:HC, ts], ps[2][HC:P, ts], ALU.mult
                                            ).then_inc(mult_done[1], 1)
                    eng.wait_ge(act_hi[1], half_chunk_at(h, p))
                    nc.vector.tensor_tensor(act[HC:P, 1, 0, ts], work[1][0:HC, ts], act[0:HC, 1, 0, ts].bitcast(F32),
                                            ALU.subtract).then_inc(act_full[1], 1)
                eng.wait_ge(down_added, START + h * DOWNS + b * ADDS)
                eng.wait_ge(down_done, START + h * DOWNS + b * ADDS + 1)
                for p in range(NT):
                    part = acc[0:2 * Q, KT, p * TT:(p + 1) * TT]
                    nc.vector.tensor_tensor(part, part, ps[down_pair(b, 0)][0:2 * Q, p * TT:(p + 1) * TT],
                                            ALU.add).then_inc((down_t, down_added)[p], 1)
                for p in range(NT):
                    t_sum(acc[0:Q, KT, :], 1, p, DOWN_T[p], pick_half)
                for p in range(NT):
                    t_low(1, p, DOWN_T[p])
                for k in range(KT):
                    add_down(b, k + 1)
                    if k - 1 in X1_BY_VECTOR:
                        x1_low(k - 1)
                    if k in (3, 4):
                        turn_item(AFTER, AL + (k - 3), ("Al", "scale")[k - 3])
                    if k == 4:
                        turn_item(AFTER, 14, "O")
                x1_low(KT - 1)
                turn_item(AFTER, 15, "O")
                turn_item(AFTER, 16, "Bl0")
                item_full(eng, h, AFTER, 13)
                for p in range(NT):
                    t_sum(ps[0][0:Q, :], 0, p, OUT_T[p], pick_scale)
                turn_item(AFTER, 17, "Bl1")
                for p in range(NT):
                    t_low(0, p, OUT_T[p])
                turn_item(AFTER, 18, "O")
                turn_item(AFTER, 19, "O")
                eng.wait_ge(bias_loaded, NQ * 16)
                for k in range(KT):
                    if k + 4 < KT:
                        turn_item(AFTER, 20 + k, "O")
                    for p in range(NT):
                        ts, out_count = slice(p * TT, (p + 1) * TT), h * KT * NT + k * NT + p + 1
                        eng.wait_ge(out_done, START + out_count)
                        nc.vector.scalar_tensor_tensor(out=acc[:, k, ts], in0=ps[out_pair(k)][:, ts],
                                                       scalar=bias[:, k:k + 1], in1=acc[:, k, ts],
                                                       op0=ALU.add, op1=ALU.add).then_inc(out_added, 1)
                        if k % 2:
                            eng.wait_ge(out_added, START + out_count)
                            eng.wait_ge(out_stored[p], START + h * (KT // 2 * NQ * 16) + k // 2 * (NQ * 16))
                            nc.vector.transpose(
                                stage[p][:, :, :].rearrange("p t (k i) -> p t k i", k=2),
                                acc[:, k - 1:k + 1, ts].rearrange("p k (t i) -> p t k i", i=Q)
                            ).then_inc(out_turned, 1)

        @block.tensor
        def _(eng):
            for sem_ in (*wk_used[0], *wk_used[1], *unit_done[0], *unit_done[1], down_done, out_done):
                eng.sem_inc(sem_, START)
            with eng.Fori(0, HALVES) as h:
                def matmul(dst, stationary, moving, start=False, stop=False):
                    return nc.tensor.matmul(dst, stationary, moving, start=start, stop=stop)

                def tok(p):
                    return slice(p * TT, (p + 1) * TT)

                def three(dst, w_hi, w_lo, moving, start=False, stop=False, pairs=range(NT)):
                    for p in pairs:
                        matmul(dst[:, tok(p)], w_hi, moving[0][:, tok(p)], start=start)
                    for p in pairs:
                        matmul(dst[:, tok(p)], w_hi, moving[1][:, tok(p)])
                    for p in pairs:
                        last = matmul(dst[:, tok(p)], w_lo, moving[0][:, tok(p)], stop=stop)
                    return last

                def tiles(dst, j, ks, pairs=range(NT), stop=False):
                    for k in ks:
                        last = three(dst, Wk[j][:, 0, k, :], Wk[j][:, 1, k, :], [X[:, 0, k, :], X[:, 1, k, :]],
                                     start=(k == 0), stop=(stop and k == KT - 1), pairs=pairs)
                    return last

                def over_width(dst, j, items):
                    for g in range(2):
                        for item in items:
                            item_full(eng, h, *item, granules=g + 1)
                        tiles(dst, j, range(4 * g, 4 * g + 4)).then_inc(wk_used[j][g], 1)

                def t_there(part):
                    eng.wait_ge(t_full, h * T_PARTS + part)
                    eng.wait_ge(t_again, h * T_PARTS + part)

                def adapter(dst, stationary, moving, p, stop=True):
                    return matmul(dst[:, tok(p)], stationary, moving[:, tok(p)], stop=stop)

                def adapters(dst, w, c, parts):
                    for p in range(NT):
                        t_there(parts[p])
                        last = adapter(dst, Bf[:, w, c, p, :], Tm[w], p)
                    last.then_inc(unit_done[w][c], 1)

                def units(c, b, items, b_items):
                    for w in range(2):
                        if c == 0:
                            eng.wait_ge(silu_done[0] if w == 0 else mult_done[0], chunk_at(h, 0, b))
                        else:
                            eng.wait_ge(down_added, START + h * DOWNS + b * ADDS - 1 + w)
                            eng.wait_ge(t_summed, h * T_PARTS + 2 * NT)
                        over_width(ps[2 * c + w], w, [items[w]])
                        item_full(eng, h, *b_items[w], granules=c + 1)
                        adapters(ps[2 * c + w], w, c, (GATE_T, UP_T)[w])

                def a_down(dst, c, half, stop):
                    for p in range(NT):
                        stationary = Ad[:, c, p, :, :].rearrange("p l r -> p (l r)")
                        parts = 1 if half else 2
                        for l in range(parts):
                            last = matmul(dst[0:2 * Q, tok(p)], stationary, act[:, c, l, tok(p)],
                                          start=(c == 0 and l == 0), stop=(stop and l == parts - 1))
                    return last

                def down_tile(dst, k, c, stop=False):
                    return three(dst, Wd[:, c, 0, k, :], Wd[:, c, 1, k, :], [act[:, c, 0, :], act[:, c, 1, :]],
                                 start=(c == 0), stop=stop)

                def down_tile_half(dst, k):
                    for p in range(NT):
                        matmul(dst[:, tok(p)], Wd[:, 1, 0, k, :], act[:, 1, 0, tok(p)])
                    for p in range(NT):
                        matmul(dst[:, tok(p)], Wd[0:HC, 1, 1, k, :], act[0:HC, 1, 0, tok(p)])

                def turn(s, b):
                    units(1, b, [(s, -2), (s, -1)], [(s, -5), (s, -3)])
                    units(0, b + 1, [(s, 2), (s, 4)], [(s, 3), (s, 5)])
                    for c in range(2):
                        eng.wait_ge(act_full[c], chunk_at(h, c, b + 1))
                    eng.wait_ge(ad_full, START + h * BLOCKS + b + 1)
                    item_full(eng, h, s, 0)
                    item_full(eng, h, s, 1)
                    for i in range(ADDS):
                        dst = ps[down_pair(b, i)]
                        if i < 2:
                            eng.wait_ge((mult_done, silu_done)[i][1], chunk_at(h, 1, b + 1))
                        else:
                            eng.wait_ge(down_added, START + h * DOWNS + b * ADDS + (i - 1))
                        for c in range(2):
                            done = (a_down(dst, c, False, c == 1) if i == 0 else
                                    down_tile(dst, i - 1, c, stop=(c == 1)))
                        done.then_inc(down_done, 1)

                def a_gate_up(p, kq):
                    item_full(eng, h, BEFORE, AGU[p], granules=kq + 1)
                    for k in range(4 * kq, 4 * kq + 4):
                        x_loaded(p, k)
                        for l in range(2):
                            last = matmul(ps[2][:, tok(p)], Wd[:, 1, p, k, :], X[:, l, k, tok(p)],
                                          start=(k == 0 and l == 0), stop=(k == KT - 1 and l == 1))
                    return last

                def x_loaded(p, k):
                    if k % 2 == 0:
                        for n in X_AT[k // 4 * 4 + 2 * p:k // 4 * 4 + 2 * p + 2]:
                            item_full(eng, h, BEFORE, n, granules=k % 4 // 2 + 1)

                def first_unit(w, p, kq):
                    item_full(eng, h, BEFORE, FIRST_ITEMS.index("GU"[w]), granules=kq + 1)
                    for k in range(4 * kq, 4 * kq + 4):
                        x_loaded(p, k)
                        last = tiles(ps[w], w, [k], pairs=[p])
                    return last

                eng.wait_ge(out_added, START + h * KT * NT)
                for p in range(NT):
                    for w in range(2):
                        last = first_unit(w, p, 0)
                        if p == NT - 1:
                            last.then_inc(wk_used[w][0], 1)
                    a_gate_up(p, 0)
                for p in range(NT):
                    a_gate_up(p, 1).then_inc(a_products, 1)
                    last = first_unit(0, p, 1)
                last.then_inc(wk_used[0][1], 1)
                for p in range(NT):
                    last = first_unit(1, p, 1)
                last.then_inc(wk_used[1][1], 1)
                for w in range(2):
                    item_full(eng, h, BEFORE, FIRST_ITEMS.index(("Bg", "Bu")[w]))
                    adapters(ps[w], w, 0, (GATE_T, UP_T)[w])
                with eng.Fori(0, TURNS) as s:
                    turn(s, s)
                turn(AFTER, TURNS)

                b = BLOCKS - 1
                base = h * DOWNS + b * ADDS
                eng.wait_ge(down_added, START + base - 1)
                for p in range(NT):
                    for g in range(2):
                        item_full(eng, h, AFTER, 6, granules=g + 1)
                        item_full(eng, h, AFTER, 7, granules=g + 1)
                        last = tiles(ps[2], 0, range(4 * g, 4 * g + 4), pairs=[p])
                        if p == NT - 1:
                            last.then_inc(wk_used[0][g], 1)
                    adapter(ps[2], Bf[:, 0, 1, p, :], Tm[0], p, stop=False).then_inc(unit_done[0][1], 1)
                    adapter(ps[2], Bf[:, 1, 1, p, :], Tm[1], p).then_inc(unit_done[1][1], 1)

                eng.wait_ge(act_full[0], chunk_at(h, 0, BLOCKS))
                eng.wait_ge(ad_full, START + h * BLOCKS + BLOCKS)
                item_full(eng, h, AFTER, 8)
                eng.wait_ge(down_added, START + base)
                a_down(ps[3], 0, False, False)
                eng.wait_ge(silu_done[0], chunk_at(h, 0, BLOCKS))
                down_tile(ps[0], 0, 0)
                eng.wait_ge(mult_done[0], chunk_at(h, 0, BLOCKS))
                down_tile(ps[1], 1, 0)
                eng.wait_ge(mult_done[1], chunk_at(h, 1, BLOCKS + NT - 1))
                down_tile(ps[2], 2, 0)
                eng.wait_ge(act_full[1], chunk_at(h, 1, BLOCKS + NT - 1))
                item_full(eng, h, AFTER, 9)
                a_down(ps[3], 1, True, True).then_inc(down_done, 1)
                for k in range(3):
                    down_tile_half(ps[down_pair(b, k + 1)], k)
                for k in range(3, KT):
                    dst = ps[down_pair(b, k + 1)]
                    eng.wait_ge(down_added, START + base + (k - 2))
                    down_tile(dst, k, 0)
                    down_tile_half(dst, k)
                    if k == 3:
                        item_full(eng, h, AFTER, 10)
                        item_full(eng, h, AFTER, 11)
                    for p in range(NT):
                        t_there(DOWN_T[p])
                        for t in (range(4) if k == 3 else [k]):
                            last = adapter(ps[down_pair(b, t + 1)], Wk[0][0:3 * Q, p, t, :], Tm[1], p)
                            if p == NT - 1:
                                last.then_inc(down_done, 1)

                eng.wait_ge(down_added, START + base + 6)
                item_full(eng, h, AFTER, AL)
                for k in range(KT):
                    by_dve = k in X1_BY_VECTOR
                    mine = [t for t in range(KT) if (t in X1_BY_VECTOR) == by_dve]
                    eng.wait_ge(x1_full[by_dve], h * len(mine) + (mine.index(k) + 1))
                    for p in range(NT):
                        for l in range(2):
                            last = matmul(ps[0][0:2 * Q, tok(p)], Wk[1][:, 0, k, p * 2 * Q:(p + 1) * 2 * Q],
                                          X[:, l, k, tok(p)], start=(k == 0 and l == 0),
                                          stop=(k == KT - 1 and l == 1))
                        if k == KT - 1 and p == 0:
                            last.then_inc(a_products, 1)
                    if k % 4 == 3:
                        last.then_inc(wk_used[1][k // 4], 1)
                for k in range(KT):
                    dst = ps[out_pair(k)]
                    if k < 3:
                        eng.wait_ge(down_added, START + base + (7 + k))
                    elif k == 3:
                        eng.wait_ge(t_summed, h * T_PARTS + OUT_T[-1])
                    else:
                        eng.wait_ge(out_added, START + h * KT * NT + (k - 3) * NT)
                    for p in range(NT):
                        for g in range(2):
                            item_full(eng, h, AFTER, 14 + k + (2 if k >= 2 else 0), granules=g + 1)
                            last = tiles(dst, k % 2, range(4 * g, 4 * g + 4), pairs=[p])
                            if p == NT - 1:
                                last.then_inc(wk_used[k % 2][g], 1)
                        if k == 2 and p == 0:
                            for q in range(NT):
                                t_there(OUT_T[q])
                                item_full(eng, h, AFTER, 16 + q)
                            for t in range(2):
                                for q in range(NT):
                                    adapter(ps[out_pair(t)], Wd[0:3 * Q, 0, q, t, :], Tm[0], q
                                            ).then_inc(out_done, 1)
                        if k >= 2:
                            adapter(dst, Wd[0:3 * Q, 0, p, k, :], Tm[0], p).then_inc(out_done, 1)


_INS = ["x", "itok_B_2_6", "itok_B_1_7", "L0_cond_W_gate", "L0_cond_W_up", "L0_cond_W_down",
        "L0_cond_A_gate", "L0_cond_B_gate", "L0_cond_A_up", "L0_cond_B_up", "L0_cond_A_down", "L0_cond_B_down",
        "L1_cond_weight", "L1_cond_bias", "L1_cond_lora_a_weights", "L1_cond_lora_b_weights",
        "L1_cond_scaling_factors"]
_OUTS = [((8, 256, 1024), "float32")]


def kernel(**inputs):
    import numpy as _np
    import concourse.bacc as _bacc
    from concourse import mybir as _mybir
    from concourse.bass_utils import run_bass_kernel_spmd as _run

    nc = _bacc.Bacc("TRN2", target_bir_lowering=False, num_devices=1)
    arrays, args = {}, []
    for name in _INS:
        a = _np.ascontiguousarray(inputs[name])
        arrays[f"in_{name}_dram"] = a
        args.append(nc.dram_tensor(f"in_{name}_dram", a.shape, _mybir.dt.from_np(a.dtype), kind="ExternalInput").ap())
    for i, (shape, dtype) in enumerate(_OUTS):
        dt = _mybir.dt.from_np(_np.dtype(dtype))
        args.append(nc.dram_tensor(f"out_{i}_dram", shape, dt, kind="ExternalOutput").ap())
    build(nc, *args)
    r = _run(nc, [arrays], core_ids=[0])
    return r.results[0]["out_0_dram"]
```
